# Optimizing a Trainium2 kernel written in Bass

```python
import numpy as np
import jax
import jax.numpy as jnp

def _softmax(x, axis=-1):
    return jax.nn.softmax(x, axis=axis)

def _gelu(x):
    return jax.nn.gelu(x, approximate=True)

def _silu(x):
    return jax.nn.silu(x)

def _sigmoid(x):
    return jax.nn.sigmoid(x)

def _layernorm(x, axis=-1, eps=1e-05):
    m = jnp.mean(x, axis=axis, keepdims=True)
    v = jnp.var(x, axis=axis, keepdims=True)
    return (x - m) / jnp.sqrt(v + eps)

def _scatter_add(tgt, idx, src, axis=0):
    return tgt.at[idx].add(src)

def _segment_sum(src, seg, n):
    return jax.ops.segment_sum(src, seg, n)
kernel_name = 'mk_xattn_ffn_d2_seqx_r4_05dbab'

def setup_inputs(seed: int=0):
    np.random.seed(seed)
    _w = jnp.asarray

    def _rec_inputs():
        import jax
        import jax.numpy as jnp
        _rk = jax.random.key(seed)
        x = 7.22e-05 + 1 * jax.random.normal(jax.random.fold_in(_rk, 1), (4, 512, 256), jnp.float32)
        _lenS = 512 - jax.random.randint(jax.random.fold_in(_rk, 7), (4,), 0, max(1, 512 // 4) + 1, jnp.int32)
        _lenS2 = 1024 - jax.random.randint(jax.random.fold_in(_rk, 8), (4,), 0, max(1, 1024 // 4) + 1, jnp.int32)
        _ctx_1024P = jax.random.normal(jax.random.fold_in(_rk, 11), (4, 16, 256), jnp.float32)
        _ctx_1024c = jax.random.dirichlet(jax.random.fold_in(_rk, 511), 0.3 * jnp.ones((16,), jnp.float32), (4, 1024))
        _ctx_1024t = jnp.einsum('bsk,bkd->bsd', _ctx_1024c, _ctx_1024P)
        _ctx_1024t = _ctx_1024t * jax.lax.rsqrt(jnp.mean(jnp.square(_ctx_1024t)) + 1e-12) * 0.953939
        ctx_1024 = -0.000514642 + 1.00011 * (_ctx_1024t + 0.3 * jax.random.normal(jax.random.fold_in(_rk, 611), (4, 1024, 256), jnp.float32))
        _validS = jnp.arange(512)[None, :] < _lenS[:, None]
        _validS2 = jnp.arange(1024)[None, :] < _lenS2[:, None]
        _causal = jnp.tril(jnp.ones((512, 512), dtype=bool))
        mask_BxSxS2_bf1 = jnp.ones((4, 512, 1024), dtype=bool)
        return (x, ctx_1024, mask_BxSxS2_bf1)
    x, ctx_1024, mask_BxSxS2_bf1 = _rec_inputs()

    def _L0_xattn_setup():
        import jax, jax.numpy as jnp
        import numpy as np
        B, L_ENC, L_DEC, D = (16, 128, 128, 256)
        key = jax.random.key(seed)
        k1, k2, k3, k4, k5, k6 = jax.random.split(key, 6)
        encoder_hc = jax.random.normal(k1, (B, L_ENC, D), dtype=jnp.float32)
        decoder_hq = jax.random.normal(k2, (B, L_DEC, D), dtype=jnp.float32)
        w_sim = jax.random.normal(k3, (3 * D,), dtype=jnp.float32) * 0.02
        b_sim = jax.random.normal(k4, (1,), dtype=jnp.float32) * 0.02
        W_qv = jax.random.normal(k5, (4 * D, D), dtype=jnp.float32) * 0.02
        b_qv = jax.random.normal(k6, (D,), dtype=jnp.float32) * 0.02
        return {'encoder_hc': encoder_hc, 'decoder_hq': decoder_hq, 'w_sim': w_sim, 'b_sim': b_sim, 'W_qv': W_qv, 'b_qv': b_qv}
    _L0_xattn_all = _L0_xattn_setup()
    _L0_xattn_in = {k: v for k, v in _L0_xattn_all.items() if k in ('w_sim', 'b_sim', 'W_qv', 'b_qv')}
    del _L0_xattn_all

    def _L0_ffn_setup():
        import jax, jax.numpy as jnp
        import numpy as np
        B, S, D = (2, 512, 256)
        DFF = 512
        E_FFN = 8
        E_ZERO = 4
        E_TOT = E_FFN + E_ZERO
        TOP_K = 2
        key = jax.random.key(seed)
        k1, k2, k3, k4 = jax.random.split(key, 4)
        x = jax.random.normal(k1, (B, S, D), dtype=jnp.float32)
        gate_w = jax.random.normal(k2, (E_TOT, D), dtype=jnp.float32) * (1.0 / np.sqrt(D))
        expert_bias = jnp.zeros((E_TOT,), dtype=jnp.float32)
        w1 = jax.random.normal(k3, (E_FFN, DFF, D), dtype=jnp.float32) * (1.0 / np.sqrt(D))
        w2 = jax.random.normal(k4, (E_FFN, D, DFF), dtype=jnp.float32) * (1.0 / np.sqrt(DFF))
        return {'x': x, 'gate_w': gate_w, 'expert_bias': expert_bias, 'w1': w1, 'w2': w2}
    _L0_ffn_all = _L0_ffn_setup()
    _L0_ffn_in = {k: v for k, v in _L0_ffn_all.items() if k in ('gate_w', 'expert_bias', 'w1', 'w2')}
    del _L0_ffn_all

    def _L1_xattn_setup():
        import jax, jax.numpy as jnp
        import numpy as np
        DIM = 256
        HEAD_DIM = 64
        NUM_HEADS = DIM // HEAD_DIM
        SCALE = HEAD_DIM ** (-0.5)
        key = jax.random.key(seed)
        k_x, k_ctx, k_wq, k_wkv, k_wo = jax.random.split(key, 5)
        B, N, M = (2, 512, 512)
        x = jax.random.normal(k_x, (B, N, DIM), dtype=jnp.float32)
        context = jax.random.normal(k_ctx, (B, M, DIM), dtype=jnp.float32)
        mask = jnp.ones((B, N, M), dtype=bool)
        s = DIM ** (-0.5)
        Wq = jax.random.normal(k_wq, (DIM, DIM), dtype=jnp.float32) * s
        Wkv = jax.random.normal(k_wkv, (DIM, 2 * DIM), dtype=jnp.float32) * s
        Wo = jax.random.normal(k_wo, (DIM, DIM), dtype=jnp.float32) * s
        return {'x': x, 'context': context, 'mask': mask, 'Wq': Wq, 'Wkv': Wkv, 'Wo': Wo}
    _L1_xattn_all = _L1_xattn_setup()
    _L1_xattn_in = {k: v for k, v in _L1_xattn_all.items() if k in ('Wq', 'Wkv', 'Wo')}
    del _L1_xattn_all

    def _L1_ffn_setup():
        import jax, jax.numpy as jnp
        import numpy as np
        TOP_K = 2
        LN_EPS = 1e-05
        B, S, H, E, F = (2, 512, 256, 8, 1024)

        def _layernorm(x, w, b):
            mu = jnp.mean(x, axis=-1, keepdims=True)
            var = jnp.mean(jnp.square(x - mu), axis=-1, keepdims=True)
            return (x - mu) * jax.lax.rsqrt(var + LN_EPS) * w + b
        key = jax.random.key(seed)
        ks = jax.random.split(key, 6)
        x = jax.random.normal(ks[0], (B, S, H), dtype=jnp.float32)
        Wg = jax.random.normal(ks[1], (H, E), dtype=jnp.float32) * 0.02
        alpha = jax.random.normal(ks[2], (E,), dtype=jnp.float32)
        ln_w = jnp.ones((E, H), dtype=jnp.float32)
        ln_b = jnp.zeros((E, H), dtype=jnp.float32)
        fc1_w = jax.random.normal(ks[3], (E, H, F), dtype=jnp.float32) * 0.02
        fc1_b = jnp.zeros((E, F), dtype=jnp.float32)
        fc2_w = jax.random.normal(ks[4], (E, F, H), dtype=jnp.float32) * 0.02
        fc2_b = jnp.zeros((E, H), dtype=jnp.float32)
        return {'x': x, 'Wg': Wg, 'alpha': alpha, 'ln_w': ln_w, 'ln_b': ln_b, 'fc1_w': fc1_w, 'fc1_b': fc1_b, 'fc2_w': fc2_w, 'fc2_b': fc2_b}
    _L1_ffn_all = _L1_ffn_setup()
    _L1_ffn_in = {k: v for k, v in _L1_ffn_all.items() if k in ('Wg', 'alpha', 'ln_w', 'ln_b', 'fc1_w', 'fc1_b', 'fc2_w', 'fc2_b')}
    del _L1_ffn_all
    return {'x': x, 'ctx_1024': ctx_1024, 'mask_BxSxS2_bf1': mask_BxSxS2_bf1, 'L0_xattn_w_sim': _L0_xattn_in['w_sim'], 'L0_xattn_b_sim': _L0_xattn_in['b_sim'], 'L0_xattn_W_qv': _L0_xattn_in['W_qv'], 'L0_xattn_b_qv': _L0_xattn_in['b_qv'], 'L0_ffn_gate_w': _L0_ffn_in['gate_w'], 'L0_ffn_expert_bias': _L0_ffn_in['expert_bias'], 'L0_ffn_w1': _L0_ffn_in['w1'], 'L0_ffn_w2': _L0_ffn_in['w2'], 'L1_xattn_Wq': _L1_xattn_in['Wq'], 'L1_xattn_Wkv': _L1_xattn_in['Wkv'], 'L1_xattn_Wo': _L1_xattn_in['Wo'], 'L1_ffn_Wg': _L1_ffn_in['Wg'], 'L1_ffn_alpha': _L1_ffn_in['alpha'], 'L1_ffn_ln_w': _L1_ffn_in['ln_w'], 'L1_ffn_ln_b': _L1_ffn_in['ln_b'], 'L1_ffn_fc1_w': _L1_ffn_in['fc1_w'], 'L1_ffn_fc1_b': _L1_ffn_in['fc1_b'], 'L1_ffn_fc2_w': _L1_ffn_in['fc2_w'], 'L1_ffn_fc2_b': _L1_ffn_in['fc2_b']}

def reference(x, ctx_1024, mask_BxSxS2_bf1, L0_xattn_w_sim, L0_xattn_b_sim, L0_xattn_W_qv, L0_xattn_b_qv, L0_ffn_gate_w, L0_ffn_expert_bias, L0_ffn_w1, L0_ffn_w2, L1_xattn_Wq, L1_xattn_Wkv, L1_xattn_Wo, L1_ffn_Wg, L1_ffn_alpha, L1_ffn_ln_w, L1_ffn_ln_b, L1_ffn_fc1_w, L1_ffn_fc1_b, L1_ffn_fc2_w, L1_ffn_fc2_b):
    import jax
    import jax.numpy as jnp

    def _L0_xattn_ref(encoder_hc, decoder_hq, w_sim, b_sim, W_qv, b_qv):
        import jax, jax.numpy as jnp
        import numpy as np
        B, L_ENC, L_DEC, D = (16, 128, 128, 256)
        d = encoder_hc.shape[-1]
        w1, w2, w3 = (w_sim[:d], w_sim[d:2 * d], w_sim[2 * d:])
        Sim = (encoder_hc @ w1)[:, :, None] + (decoder_hq @ w2)[:, None, :] + jnp.einsum('bid,bjd->bij', encoder_hc * w3, decoder_hq) + b_sim[0]
        A = jax.nn.softmax(Sim, axis=2)
        hq_hat = jnp.einsum('bij,bjd->bid', A, decoder_hq)
        Batt = jax.nn.softmax(jnp.max(Sim, axis=2), axis=1)
        hc_bar = jnp.einsum('bi,bid->bd', Batt, encoder_hc)[:, None, :]
        hc_hat = jnp.broadcast_to(hc_bar, encoder_hc.shape)
        feats = jnp.concatenate([encoder_hc, hq_hat, encoder_hc * hq_hat, encoder_hc * hc_hat], axis=-1)
        hcq = feats @ W_qv + b_qv
        return hcq

    def _L0_ffn_ref(x, gate_w, expert_bias, w1, w2):
        import jax, jax.numpy as jnp
        import numpy as np
        B, S, D = (2, 512, 256)
        DFF = 512
        E_FFN = 8
        E_ZERO = 4
        E_TOT = E_FFN + E_ZERO
        TOP_K = 2
        logits = jnp.einsum('btd,ed->bte', x, gate_w) + expert_bias
        topk_logits, topk_idx = jax.lax.top_k(logits, TOP_K)
        topk_w = jax.nn.softmax(topk_logits, axis=-1)
        onehot = jax.nn.one_hot(topk_idx, E_TOT, dtype=x.dtype)
        w = jnp.einsum('btk,btke->bte', topk_w, onehot)
        w_ffn = w[..., :E_FFN]
        w_zero = jnp.sum(w[..., E_FFN:], axis=-1)
        h = jax.nn.silu(jnp.einsum('btd,efd->btef', x, w1))
        y = jnp.einsum('btef,edf->bted', h, w2)
        out = jnp.einsum('bte,bted->btd', w_ffn, y) + w_zero[..., None] * x
        return out

    def _L1_xattn_ref(x, context, mask, Wq, Wkv, Wo):
        import jax, jax.numpy as jnp
        import numpy as np
        DIM = 256
        HEAD_DIM = 64
        NUM_HEADS = DIM // HEAD_DIM
        SCALE = HEAD_DIM ** (-0.5)
        B, N, C = x.shape
        M = context.shape[1]
        H, D = (NUM_HEADS, HEAD_DIM)
        q = (x @ Wq).reshape(B, N, H, D).transpose(0, 2, 1, 3)
        kv = (context @ Wkv).reshape(B, M, 2, H, D).transpose(2, 0, 3, 1, 4)
        k, v = (kv[0], kv[1])
        attn = jnp.einsum('bhnd,bhmd->bhnm', q, k) * SCALE
        attn = jnp.where(mask[:, None, :, :], attn, -jnp.inf)
        attn = jax.nn.softmax(attn, axis=-1)
        out = jnp.einsum('bhnm,bhmd->bhnd', attn, v)
        out = out.transpose(0, 2, 1, 3).reshape(B, N, C)
        return out @ Wo

    def _L1_ffn_ref(x, Wg, alpha, ln_w, ln_b, fc1_w, fc1_b, fc2_w, fc2_b):
        import jax, jax.numpy as jnp
        import numpy as np
        TOP_K = 2
        LN_EPS = 1e-05
        B, S, H, E, F = (2, 512, 256, 8, 1024)

        def _layernorm(x, w, b):
            mu = jnp.mean(x, axis=-1, keepdims=True)
            var = jnp.mean(jnp.square(x - mu), axis=-1, keepdims=True)
            return (x - mu) * jax.lax.rsqrt(var + LN_EPS) * w + b
        b, s, h = x.shape
        xf = x.reshape(-1, h)
        logits = xf @ Wg
        top_vals, top_idx = jax.lax.top_k(logits, TOP_K)
        gate_score = jax.nn.softmax(top_vals, axis=-1)
        one_hot = jax.nn.one_hot(top_idx, Wg.shape[1], dtype=xf.dtype)
        comb = jnp.einsum('tke,tk->te', one_hot, gate_score) * alpha
        out = jnp.zeros_like(xf)
        for e in range(Wg.shape[1]):
            hdn = _layernorm(xf, ln_w[e], ln_b[e])
            a = jax.nn.gelu(hdn @ fc1_w[e] + fc1_b[e], approximate=True)
            y = a @ fc2_w[e] + fc2_b[e]
            out = out + y * comb[:, e:e + 1]
        return out.reshape(b, s, h)
    x = x + _L0_xattn_ref(_layernorm(x, axis=-1), ctx_1024, L0_xattn_w_sim, L0_xattn_b_sim, L0_xattn_W_qv, L0_xattn_b_qv)
    x = x + _L0_ffn_ref(_layernorm(x, axis=-1), L0_ffn_gate_w, L0_ffn_expert_bias, L0_ffn_w1, L0_ffn_w2)
    x = x + _L1_xattn_ref(_layernorm(x, axis=-1), ctx_1024, mask_BxSxS2_bf1, L1_xattn_Wq, L1_xattn_Wkv, L1_xattn_Wo)
    x = x + _L1_ffn_ref(_layernorm(x, axis=-1), L1_ffn_Wg, L1_ffn_alpha, L1_ffn_ln_w, L1_ffn_ln_b, L1_ffn_fc1_w, L1_ffn_fc1_b, L1_ffn_fc2_w, L1_ffn_fc2_b)
    return x

_drawn_inputs = setup_inputs


def setup_inputs(seed=0):
    import zlib

    import numpy as np

    out = dict(_drawn_inputs(seed))
    spreads = {'L0_ffn_expert_bias': (0.0, 0.1),
     'L1_ffn_ln_w': (1.0, 0.6),
     'L1_ffn_ln_b': (0.0, 0.8),
     'L1_ffn_fc1_b': (0.0, 0.584),
     'L1_ffn_fc2_b': (0.0, 0.1)}
    factors = {}
    for name, (base, spread) in spreads.items():
        noise = np.random.default_rng([zlib.crc32(name.encode()), seed]).standard_normal(out[name].shape)
        drawn = base * np.exp(spread * noise) if base else spread * noise
        out[name] = jnp.asarray(drawn.astype(out[name].dtype))
    for name, factor in factors.items():
        out[name] = (out[name] * factor).astype(out[name].dtype)
    return out
```

```python
from contextlib import ExitStack

import numpy as np

import concourse.bass as bass
from concourse import mybir

F32 = mybir.dt.float32
BF16 = mybir.dt.bfloat16
I32 = mybir.dt.int32
U8 = mybir.dt.uint8
ALU = mybir.AluOpType
ACT = mybir.ActivationFunctionType
AX = mybir.AxisListType
ds = bass.ds

P = 128
B, S, D = 4, 512, 256
M = 1024
T = B * S // P
TB = S // P
KD = D // P
JC = M // P
H, HD = 4, 64
E = 8
NB = (2 * T * P - E) // P + E
NBX = NB + 1
EPS = 1e-5
BIG = 3e38
PB = 4
LANES = 3

C_IDENT = 0
C_ONES = C_IDENT + P
C_BEFORE = C_ONES + P
C_ROW = C_BEFORE + P
C_TOKEN = C_ROW + P
C_PAD = C_TOKEN + T
C_ZERO = C_PAD + 1
C_EPS = C_ZERO + 1
C_THR = C_EPS + 1
C_BLK = C_THR + T
C_EXP = C_BLK + NBX
C_END = C_EXP + 12 * T


def shape_constants():
    c = np.zeros((P, C_END), np.float32)
    p = np.arange(P)
    c[:, C_IDENT:C_IDENT + P] = np.eye(P)
    c[:, C_ONES:C_ONES + P] = 1
    c[:, C_BEFORE:C_BEFORE + P] = p[:, None] < p[None, :]
    c[:, C_ROW:C_ROW + P] = p[None, :]
    c[:, C_TOKEN:C_TOKEN + T] = p[:, None] + P * np.arange(T)[None, :] + 1
    c[:, C_PAD] = T * P + p + 1
    c[:, C_EPS] = EPS
    c[:, C_THR:C_THR + T] = P * np.arange(T)
    c[:, C_BLK:C_BLK + NBX] = np.arange(NBX)
    c[:, C_EXP:C_END] = np.repeat(np.arange(12), T)[None, :]
    return c


def apart(m, eng):
    eng.sem_inc(m.s_apart[eng is m.nc.vector], 1)


class Mem:
    pass


def load_phase(nc, m, dram):
    s_in = m.s_const
    with nc.Block() as block:
        @block.sync
        def _(sp):
            sp.dma_start(m.x[:], dram["x"].rearrange("(t p) d -> p t d", p=P)).then_inc(s_in, 16)
            sp.dma_start(m.const[:], dram["const"]).then_inc(s_in, 16)
            sp.wait_ge(s_in, 32)


def layer_norm_stats(nc, m, tag):
    with (nc.semaphore(f"{tag}_bn_done") as s_st, nc.semaphore(f"{tag}_stat_step") as s_v,
          nc.semaphore(f"{tag}_sqrt_done") as s_sq, nc.Block() as block):
        @block.vector
        def _(dve):
            with dve.Fori(0, T) as g:
                nc.vector.bn_stats(m.bn[:, ds(g, 1), :].rearrange("p a s -> p (a s)"),
                                   m.x[:, ds(g, 1), :].rearrange("p a d -> p (a d)")).then_inc(s_st, 1)
            dve.wait_ge(s_st, T)
            mean_e, m2_e, mean_o, m2_o = (m.bn[:, :, k] for k in (1, 2, 4, 5))
            nc.vector.tensor_tensor(m.mean2[:], mean_e, mean_o, ALU.add).then_inc(s_v, 1)
            nc.vector.tensor_tensor(m.diff[:], mean_e, mean_o, ALU.subtract).then_inc(s_v, 1)
            nc.vector.tensor_tensor(m.m2[:], m2_e, m2_o, ALU.add).then_inc(s_v, 1)
            dve.wait_ge(s_v, 3)
            nc.vector.tensor_scalar(m.mean[:], m.mean2[:], 0.5, None, ALU.mult).then_inc(s_v, 1)
            nc.vector.scalar_tensor_tensor(m.dd[:], m.diff[:], 0.25, m.diff[:], ALU.mult, ALU.mult).then_inc(s_v, 1)
            dve.wait_ge(s_v, 5)
            nc.vector.scalar_tensor_tensor(m.var[:], m.m2[:], 1.0 / D, m.dd[:], ALU.mult, ALU.add).then_inc(s_v, 1)
            dve.wait_ge(s_sq, 1)
            nc.vector.reciprocal(m.rstd[:], m.std[:]).then_inc(s_v, 1)

        @block.scalar
        def _(act):
            act.wait_ge(s_v, 6)
            nc.scalar.activation(m.std[:], m.var[:], ACT.Sqrt, bias=m.const[:, C_EPS:C_EPS + 1]).then_inc(s_sq, 1)


def normalise(nc, m, out, g):
    return nc.vector.tensor_scalar(out, m.x[:, ds(g, 1), :].rearrange("p a d -> p (a d)"),
                                   m.mean[:, ds(g, 1)], m.rstd[:, ds(g, 1)], ALU.subtract, ALU.mult)


def attention0(nc, m, dram):
    with ExitStack() as ctx:
        sem = lambda n: nc.alloc_semaphore(name=n)
        sb = lambda n, s, d=F32: ctx.enter_context(nc.sbuf_tensor("a_" + n, s, d))
        ps = lambda n, s: ctx.enter_context(nc.psum_tensor("a_" + n, s, F32))
        enc = [sb(f"enc{q}", [P, TB, D]) for q in range(2)]
        enc_t = [sb(f"enc_t{q}", [P, KD, S]) for q in range(2)]
        u_t = [sb(f"u_t{q}", [P, KD, S]) for q in range(2)]
        ctx_t = [sb(f"ctx_t{q}", [P, KD, M]) for q in range(2)]
        ctx_n = [sb(f"ctx_n{q}", [P, JC, D]) for q in range(2)]
        prob = [sb(f"prob{q}", [P, M]) for q in range(2)]
        prob_t = sb("prob_t", [P, JC, S])
        hq_t = sb("hq_t", [P, KD, S])
        prod_t = sb("prod_t", [P, KD, S])
        wqv = sb("wqv", [P, 4 * KD, D])
        wenc = sb("wenc", [P, KD, D])
        bqv = sb("bqv", [P, D])
        wsim = sb("wsim", [P, 3 * KD])
        bsim = sb("bsim", [P, 1])
        nmax = sb("nmax", [P, T])
        rsum = sb("rsum", [P, T])
        rinv = sb("rinv", [P, T])
        mtot = sb("mtot", [P, TB])
        mrow = sb("mrow", [P, 1])
        ngmax1 = sb("ngmax1", [1, 1])
        ngmax = sb("ngmax", [P, 1])
        bexp = sb("bexp", [P, TB])
        bsum = sb("bsum", [P, 1])
        binv = sb("binv", [P, 1])
        hc = sb("hc", [P, KD])
        upd = sb("upd", [P, TB, D])

        sc = [ps(f"sc{q}", [P, M]) for q in range(2)]
        tp = [ps(f"tp{q}", [P, S]) for q in range(2)]
        av = [ps(f"av{q}", [P, S]) for q in range(2)]
        small, proj = sc[0], sc[1]
        ident = m.const[:, C_IDENT:C_IDENT + P]
        ones = m.const[:, C_ONES:C_ONES + P]

        names = ("w_in enc_ready enc_tp enc_t_ready u_t_ready ctx_free qk_done max_done "
                 "exp_done inv_done prob_ready tp_lo tp_hi ev_lo ev_hi av_done hq_a hq_d prod_ready a_done "
                 "mtot_ready mrow_ready mrow_tp ngmax1_ready ngmax_bc ngmax_ready bexp_ready hc_done "
                 "binv_ready hc_ready wenc_ready proj_done upd_half upd_ready x_ready").split()
        s = {n: sem("a_" + n) for n in names}
        ctx_t_in = [sem(f"a_ctx_t_in{q}") for q in range(2)]
        ctx_n_in = [sem(f"a_ctx_n_in{q}") for q in range(2)]

        with nc.Block() as block:
            @block.sync
            def _(sp):
                sp.dma_start(wsim[:], dram["w_sim"]).then_inc(s["w_in"], 16)
                sp.dma_start(bsim[:], dram["b_sim"].partition_broadcast(P)).then_inc(s["w_in"], 16)
                sp.dma_start(wqv[:], dram["W_qv"].rearrange("(c p) d -> p c d", p=P)).then_inc(s["w_in"], 16)
                sp.dma_start(bqv[:], dram["b_qv"].partition_broadcast(P)).then_inc(s["w_in"], 16)
                for b in range(B):
                    if b >= 2:
                        sp.wait_ge(s["av_done"], KD * (b - 1))
                    sp.dma_start(ctx_t[b % 2][:], dram["ctx_t"][:, b * M:(b + 1) * M]
                                 .rearrange("(k p) j -> p k j", p=P)).then_inc(ctx_t_in[b % 2], 16)
                    sp.dma_start(ctx_n[b % 2][:], dram["ctx"][b * M:(b + 1) * M, :]
                                 .rearrange("(j p) d -> p j d", p=P)).then_inc(ctx_n_in[b % 2], 16)
                for e in range(E):
                    sp.dma_start(m.w1_0[:, e, :, :], dram["w1_0"][e].rearrange("(k p) f -> p k f", p=P)).then_inc(m.s_w0, 16)
                    sp.dma_start(m.w2_0[:, e, :, :], dram["w2_0"][e].rearrange("(c p) d -> p c d", p=P)).then_inc(m.s_w0, 16)

            @block.tensor
            def _(pe):
                pe.wait_ge(s["w_in"], 64)
                with pe.Fori(0, B // 2) as pair:
                    for q in range(2):
                        b, g0 = pair * 2 + q, pair * (2 * TB) + q * TB
                        pe.wait_ge(s["enc_ready"], g0 + TB)
                        pe.wait_ge(s["hq_a"], b + 1)
                        pe.wait_ge(s["hq_d"], b + 1)
                        for k in range(KD):
                            for t in range(TB):
                                mm = nc.tensor.transpose(av[k][:, t * P:(t + 1) * P],
                                                         enc[q][:, t, k * P:(k + 1) * P], ident)
                            mm.then_inc(s["enc_tp"], 1)
                        pe.wait_ge(ctx_t_in[q], pair * 16 + 16)
                        pe.wait_ge(s["u_t_ready"], b * KD + KD)
                        pe.wait_ge(s["enc_t_ready"], b * KD + KD)

                        def scores(t):
                            pe.wait_ge(s["exp_done"], g0 + t + 1)
                            if t == 1:
                                pe.wait_ge(s["upd_ready"], b + 1)
                            for half in range(2):
                                for k in range(KD):
                                    mm = nc.tensor.matmul(sc[t % 2][:, half * 512:(half + 1) * 512],
                                                          u_t[q][:, k, t * P:(t + 1) * P],
                                                          ctx_t[q][:, k, half * 512:(half + 1) * 512],
                                                          start=(k == 0), stop=(k == KD - 1))
                            mm.then_inc(s["qk_done"], 1)

                        def turn(t):
                            pe.wait_ge(s["prob_ready"], g0 + t + 1)
                            pe.wait_ge(s["ev_lo"], g0 + t + 1)
                            for j in range(JC // 2):
                                mm = nc.tensor.transpose(tp[0][:, j * P:(j + 1) * P],
                                                         prob[t % 2][:, j * P:(j + 1) * P], ident)
                            mm.then_inc(s["tp_lo"], 1)
                            pe.wait_ge(s["ev_hi"], g0 + t + 2)
                            for j in range(JC // 2):
                                mm = nc.tensor.transpose(tp[1][:, j * P:(j + 1) * P],
                                                         prob[t % 2][:, 512 + j * P:512 + (j + 1) * P], ident)
                            mm.then_inc(s["tp_hi"], 1)

                        scores(0)
                        for t in range(1, TB):
                            scores(t)
                            turn(t - 1)
                        pe.wait_ge(s["exp_done"], g0 + TB + 1)
                        for t in range(TB):
                            for k in range(KD):
                                mm = nc.tensor.matmul(small[:, t:t + 1], enc_t[q][:, k, t * P:(t + 1) * P],
                                                      wsim[:, k:k + 1], start=(k == 0), stop=(k == KD - 1))
                        mm.then_inc(s["a_done"], 1)
                        turn(TB - 1)
                        pe.wait_ge(s["mrow_ready"], b + 1)
                        nc.tensor.transpose(small[0:1, 8:8 + P], mrow[:], ident).then_inc(s["mrow_tp"], 1)
                        pe.wait_ge(ctx_n_in[q], pair * 16 + 16)
                        pe.wait_ge(s["ev_lo"], g0 + TB + 1)
                        pe.wait_ge(s["ev_hi"], g0 + TB + 2)
                        for k in range(KD):
                            for j in range(JC):
                                mm = nc.tensor.matmul(av[k][:], ctx_n[q][:, j, k * P:(k + 1) * P], prob_t[:, j, :],
                                                      start=(j == 0), stop=(j == JC - 1))
                            mm.then_inc(s["av_done"], 1)
                            if k == 0:
                                pe.wait_ge(s["ngmax1_ready"], b + 1)
                                nc.tensor.matmul(small[:, 136:137], m.const[0:1, C_ONES:C_ONES + P], ngmax1[:],
                                                 start=True, stop=True).then_inc(s["ngmax_bc"], 1)
                        pe.wait_ge(s["bexp_ready"], b + 1)
                        nc.tensor.matmul(small[:, 137:138], ones, bsum[:], start=True, stop=True)
                        for k in range(KD):
                            for t in range(TB):
                                mm = nc.tensor.matmul(small[:, 138 + k:139 + k], enc[q][:, t, k * P:(k + 1) * P],
                                                      bexp[:, t:t + 1], start=(t == 0), stop=(t == TB - 1))
                        mm.then_inc(s["hc_done"], 1)
                        pe.wait_ge(s["wenc_ready"], b + 1)
                        pe.wait_ge(s["prod_ready"], b + 1)
                        for t in range(TB):
                            ts = slice(t * P, (t + 1) * P)
                            parts = ([(hq_t[:, k, ts], wqv[:, KD + k, :]) for k in range(KD)]
                                     + [(prod_t[:, k, ts], wqv[:, 2 * KD + k, :]) for k in range(KD)]
                                     + [(enc_t[q][:, k, ts], wenc[:, k, :]) for k in range(KD)])
                            for n, (lhs, rhs) in enumerate(parts):
                                mm = nc.tensor.matmul(proj[:, t * D:(t + 1) * D], lhs, rhs,
                                                      start=(n == 0), stop=(n == len(parts) - 1))
                            if t % 2:
                                mm.then_inc(s["proj_done"], 1)

            @block.scalar
            def _(act):
                act.sem_inc(s["exp_done"], 2)
                act.sem_inc(s["ev_lo"], 1)
                act.sem_inc(s["hq_a"], 1)
                with act.Fori(0, B // 2) as pair:
                    for q in range(2):
                        b, g0 = pair * 2 + q, pair * (2 * TB) + q * TB
                        for k in range(KD):
                            act.wait_ge(s["enc_tp"], b * KD + k + 1)
                            nc.scalar.activation(enc_t[q][:, k, :], av[k][:], ACT.Copy).then_inc(s["enc_t_ready"], 1)
                        for t in range(TB):
                            g = g0 + t
                            act.wait_ge(s["max_done"], g + 1)
                            act.wait_ge(s["ev_hi"], g + 1)
                            nc.scalar.activation(prob[t % 2][:], sc[t % 2][:], ACT.Exp, bias=nmax[:, ds(g, 1)],
                                                 accum_out=rsum[:, ds(g, 1)]).then_inc(s["exp_done"], 1)
                            if t:
                                act.wait_ge(s["tp_lo"], g)
                                nc.scalar.activation(prob_t[:, 0:JC // 2, (t - 1) * P:t * P],
                                                     tp[0][:].rearrange("p (j i) -> p j i", i=P),
                                                     ACT.Copy).then_inc(s["ev_lo"], 1)
                        act.wait_ge(s["tp_lo"], g0 + TB)
                        nc.scalar.activation(prob_t[:, 0:JC // 2, (TB - 1) * P:TB * P],
                                             tp[0][:].rearrange("p (j i) -> p j i", i=P), ACT.Copy).then_inc(s["ev_lo"], 1)
                        act.wait_ge(s["ngmax_ready"], b + 1)
                        nc.scalar.activation(bexp[:], mtot[:], ACT.Exp, bias=ngmax[:],
                                             accum_out=bsum[:]).then_inc(s["bexp_ready"], 1)
                        act.wait_ge(s["av_done"], b * KD + 1)
                        nc.scalar.activation(hq_t[:, 0, :], av[0][:], ACT.Copy).then_inc(s["hq_a"], 1)

            @block.vector
            def _(dve):
                dve.sem_inc(s["ev_hi"], 2)
                dve.sem_inc(s["hq_d"], 1)
                dve.sem_inc(s["upd_ready"], 1)
                dve.sem_inc(s["x_ready"], 1)
                dve.wait_ge(s["w_in"], 64)
                with dve.Fori(0, B // 2) as pair:
                    for q in range(2):
                        b, g0 = pair * 2 + q, pair * (2 * TB) + q * TB
                        for t in range(TB):
                            normalise(nc, m, enc[q][:, t, :], g0 + t).then_inc(s["enc_ready"], 1)
                        for k in range(KD):
                            dve.wait_ge(s["enc_t_ready"], b * KD + k + 1)
                            nc.vector.tensor_scalar(u_t[q][:, k, :], enc_t[q][:, k, :], wsim[:, 2 * KD + k:2 * KD + k + 1],
                                                    wsim[:, KD + k:KD + k + 1], ALU.mult, ALU.add).then_inc(s["u_t_ready"], 1)

                        def maximum(t):
                            dve.wait_ge(s["qk_done"], g0 + t + 1)
                            nc.vector.tensor_reduce(nmax[:, ds(g0 + t, 1)], sc[t % 2][:], AX.X, ALU.max,
                                                    negate=True).then_inc(s["max_done"], 1)

                        def scale(t):
                            dve.wait_ge(s["exp_done"], g0 + t + 3)
                            nc.vector.reciprocal(rinv[:, ds(g0 + t, 1)], rsum[:, ds(g0 + t, 1)]).then_inc(s["inv_done"], 1)
                            dve.wait_ge(s["inv_done"], g0 + t + 1)
                            nc.vector.tensor_scalar(prob[t % 2][:], prob[t % 2][:], rinv[:, ds(g0 + t, 1)], None,
                                                    ALU.mult).then_inc(s["prob_ready"], 1)

                        def evict(t):
                            dve.wait_ge(s["tp_hi"], g0 + t + 1)
                            nc.vector.tensor_copy(prob_t[:, JC // 2:JC, t * P:(t + 1) * P],
                                                  tp[1][:].rearrange("p (j i) -> p j i", i=P)).then_inc(s["ev_hi"], 1)

                        maximum(0)
                        for t in range(TB):
                            if t + 1 < TB:
                                maximum(t + 1)
                            scale(t)
                            if t >= 1:
                                evict(t - 1)
                        dve.wait_ge(s["a_done"], b + 1)
                        dve.wait_ge(s["max_done"], g0 + TB)
                        nc.vector.scalar_tensor_tensor(mtot[:], small[:, 0:TB], bsim[:, 0:1], nmax[:, ds(g0, TB)],
                                                       ALU.add, ALU.subtract).then_inc(s["mtot_ready"], 1)
                        dve.wait_ge(s["mtot_ready"], b + 1)
                        nc.vector.tensor_reduce(mrow[:], mtot[:], AX.X, ALU.max).then_inc(s["mrow_ready"], 1)
                        evict(TB - 1)
                        dve.wait_ge(s["mrow_tp"], b + 1)
                        nc.vector.tensor_reduce(ngmax1[:], small[0:1, 8:8 + P], AX.X, ALU.max,
                                                negate=True).then_inc(s["ngmax1_ready"], 1)
                        dve.wait_ge(s["ngmax_bc"], b + 1)
                        nc.vector.tensor_copy(ngmax[:], small[:, 136:137]).then_inc(s["ngmax_ready"], 1)
                        dve.wait_ge(s["av_done"], b * KD + 2)
                        nc.vector.tensor_copy(hq_t[:, 1, :], av[1][:]).then_inc(s["hq_d"], 1)
                        dve.wait_ge(s["hc_done"], b + 1)
                        nc.vector.reciprocal(binv[:], small[:, 137:138]).then_inc(s["binv_ready"], 1)
                        dve.wait_ge(s["binv_ready"], b + 1)
                        nc.vector.tensor_scalar(hc[:], small[:, 138:138 + KD], binv[:], None, ALU.mult).then_inc(s["hc_ready"], 1)
                        dve.wait_ge(s["hc_ready"], b + 1)
                        for k in range(KD):
                            op = nc.vector.scalar_tensor_tensor(wenc[:, k, :], wqv[:, 3 * KD + k, :], hc[:, k:k + 1],
                                                                wqv[:, k, :], ALU.mult, ALU.add)
                        op.then_inc(s["wenc_ready"], 1)
                        for half in range(2):
                            h2 = slice(2 * half, 2 * half + 2)
                            dve.wait_ge(s["proj_done"], 2 * b + half + 1)
                            dve.wait_ge(s["x_ready"], 2 * b + half + 1)
                            op = nc.vector.tensor_tensor(upd[:, h2, :], proj[:, half * 2 * D:(half + 1) * 2 * D]
                                                         .rearrange("p (t d) -> p t d", d=D),
                                                         bqv[:].unsqueeze(1).broadcast_to([P, 2, D]), ALU.add)
                            if half:
                                op.then_inc(s["upd_ready"], 1)
                                dve.wait_ge(s["upd_ready"], b + 2)
                            else:
                                op.then_inc(s["upd_half"], 1)
                                dve.wait_ge(s["upd_half"], b + 1)
                            nc.vector.tensor_tensor(m.x[:, ds(g0 + 2 * half, 2), :], m.x[:, ds(g0 + 2 * half, 2), :],
                                                    upd[:, h2, :], ALU.add).then_inc(s["x_ready"], 1)

            @block.gpsimd
            def _(pool):
                with pool.Fori(0, B // 2) as pair:
                    for q in range(2):
                        b = pair * 2 + q
                        pool.wait_ge(s["hq_a"], b + 2)
                        pool.wait_ge(s["hq_d"], b + 2)
                        nc.gpsimd.tensor_tensor(prod_t[:], enc_t[q][:], hq_t[:], ALU.mult).then_inc(s["prod_ready"], 1)


def attention1(nc, m, dram):
    with ExitStack() as ctx:
        sem = lambda n: nc.alloc_semaphore(name=n)
        sb = lambda n, s, d=F32: ctx.enter_context(nc.sbuf_tensor("c_" + n, s, d))
        ps = lambda n, s: ctx.enter_context(nc.psum_tensor("c_" + n, s, F32))
        xn = [sb(f"xn{q}", [P, TB, D]) for q in range(2)]
        xn_t = sb("xn_t", [P, KD, S])
        ctx_t = [sb(f"ctx_t{q}", [P, KD, M]) for q in range(2)]
        mask = [sb(f"mask{q}", [P, TB, M], U8) for q in range(2)]
        mfin = sb("mfin", [P, TB, M], BF16)
        minf = sb("minf", [P, TB, M], BF16)
        q_t = sb("q_t", [P, KD, S])
        k_t = sb("k_t", [P, KD, M])
        v = sb("v", [P, JC, D])
        prob = [sb(f"prob{q}", [P, M]) for q in range(PB)]
        prob_t = sb("prob_t", [P, JC, S])
        att_t = sb("att_t", [P, KD, S])
        wq = sb("wq", [P, KD, D])
        wkv = sb("wkv", [P, KD, 2 * D])
        wo = sb("wo", [P, KD, D])
        UB = H * TB
        max_ = sb("max", [P, PB])
        nmax = sb("nmax", [P, PB])
        rsum = sb("rsum", [P, PB])
        rinv = sb("rinv", [P, PB])

        sc = [ps(f"sc{q}", [P, M]) for q in range(2)]
        tp = [ps(f"tp{q}", [P, S]) for q in range(2)]
        av = [ps(f"av{q}", [P, S]) for q in range(2)]
        proj = sc[1]
        ident = m.const[:, C_IDENT:C_IDENT + P]

        names = ("w_in mfin_ready minf_ready xn_ready xn_tp xn_ev_a xn_ev_d q_done q_ready "
                 "kv_done k_ready v_a v_d qk_done max_done nmax_ready exp_done inv_done prob_ready "
                 "tp_lo tp_hi ev_lo ev_hi av_done att_ready proj_done x_ready").split()
        s = {n: sem("c_" + n) for n in names}
        ctx_t_in = [sem(f"c_ctx_t_in{q}") for q in range(2)]
        mask_in = [sem(f"c_mask_in{q}") for q in range(2)]

        with nc.Block() as block:
            @block.sync
            def _(sp):
                sp.dma_start(wq[:], dram["Wq"].rearrange("(k p) d -> p k d", p=P)).then_inc(s["w_in"], 16)
                sp.dma_start(wkv[:], dram["Wkv"].rearrange("(k p) d -> p k d", p=P)).then_inc(s["w_in"], 16)
                sp.dma_start(wo[:], dram["Wo"].rearrange("(k p) d -> p k d", p=P)).then_inc(s["w_in"], 16)
                for b in range(B):
                    if b >= 2:
                        sp.wait_ge(s["v_d"], b - 1)
                        sp.wait_ge(s["v_a"], b - 1)
                        sp.wait_ge(s["mfin_ready"], b - 1)
                    sp.dma_start(ctx_t[b % 2][:], dram["ctx_t"][:, b * M:(b + 1) * M]
                                 .rearrange("(k p) j -> p k j", p=P)).then_inc(ctx_t_in[b % 2], 16)
                    sp.dma_start(mask[b % 2][:], dram["mask"][b * S:(b + 1) * S, :]
                                 .rearrange("(t p) j -> p t j", p=P)).then_inc(mask_in[b % 2], 16)
                for e in range(E):
                    sp.dma_start(m.w2_1[:, e, :, :], dram["w2_1"][e].rearrange("(c p) d -> p c d", p=P)).then_inc(m.s_w2, 16)

            @block.gpsimd
            def _(pool):
                pool.sem_inc(s["minf_ready"], 1)
                with pool.Fori(0, B // 2) as pair:
                    for q in range(2):
                        b = pair * 2 + q
                        pool.wait_ge(mask_in[q], pair * 16 + 16)
                        pool.wait_ge(s["minf_ready"], b + 1)
                        apart(m, pool)
                        nc.gpsimd.tensor_scalar(mfin[:], mask[q][:], -1.0, BIG, ALU.add, ALU.mult).then_inc(s["mfin_ready"], 1)
                        pool.wait_ge(s["mfin_ready"], b + 1)
                        pool.wait_ge(s["att_ready"], b * KD + KD)
                        apart(m, pool)
                        nc.gpsimd.tensor_scalar(minf[:], mfin[:], 10.0, 1.0, ALU.mult, ALU.mult).then_inc(s["minf_ready"], 1)

            @block.tensor
            def _(pe):
                pe.wait_ge(s["w_in"], 48)
                with pe.Fori(0, B // 2) as pair:
                    for q in range(2):
                        b, g0 = pair * 2 + q, pair * (2 * TB) + q * TB
                        u0 = pair * (2 * UB) + q * UB
                        pe.wait_ge(s["xn_ready"], g0 + TB)
                        pe.wait_ge(s["att_ready"], b * KD + KD)
                        for k in range(KD):
                            for t in range(TB):
                                mm = nc.tensor.transpose(av[k][:, t * P:(t + 1) * P], xn[q][:, t, k * P:(k + 1) * P], ident)
                            mm.then_inc(s["xn_tp"], 1)
                        pe.wait_ge(ctx_t_in[q], pair * 16 + 16)
                        pe.wait_ge(s["exp_done"], u0 + 2)
                        pe.wait_ge(s["x_ready"], b * 2 + 2)
                        for c in range(KD):
                            for half in range(2):
                                hs = slice(half * 512, (half + 1) * 512)
                                for k in range(KD):
                                    mm = nc.tensor.matmul(sc[c][:, hs], wkv[:, k, c * P:(c + 1) * P], ctx_t[q][:, k, hs],
                                                          start=(k == 0), stop=(k == KD - 1))
                            mm.then_inc(s["kv_done"], 1)
                        pe.wait_ge(s["xn_ev_a"], b + 1)
                        pe.wait_ge(s["xn_ev_d"], b + 1)
                        for c in range(KD):
                            for k in range(KD):
                                mm = nc.tensor.matmul(av[c][:], wq[:, k, c * P:(c + 1) * P], xn_t[:, k, :],
                                                      start=(k == 0), stop=(k == KD - 1))
                            mm.then_inc(s["q_done"], 1)
                        for c in range(2):
                            pe.wait_ge(s["k_ready"], b * KD + KD)
                            for j in range(JC // 2):
                                for k in range(KD):
                                    jj = c * (JC // 2) + j
                                    mm = nc.tensor.matmul(sc[c][:, j * D:(j + 1) * D], ctx_t[q][:, k, jj * P:(jj + 1) * P],
                                                          wkv[:, k, D:2 * D], start=(k == 0), stop=(k == KD - 1))
                            mm.then_inc(s["kv_done"], 1)
                        pe.wait_ge(s["q_ready"], b * KD + KD)

                        def scores(u):
                            h, t = divmod(u, TB)
                            rows = slice((h % 2) * HD, (h % 2 + 1) * HD)
                            if u == 0:
                                pe.wait_ge(s["v_a"], b + 1)
                            elif u == 1:
                                pe.wait_ge(s["v_d"], b + 1)
                            else:
                                pe.wait_ge(s["max_done"], u0 + u - 1)
                            for half in range(2):
                                hs = slice(half * 512, (half + 1) * 512)
                                mm = nc.tensor.matmul(sc[t % 2][:, hs], q_t[rows, h // 2, t * P:(t + 1) * P],
                                                      k_t[rows, h // 2, hs], start=True, stop=True)
                            mm.then_inc(s["qk_done"], 1)

                        def turn(u):
                            pe.wait_ge(s["prob_ready"], u0 + u + 1)
                            pe.wait_ge(s["ev_lo"], u0 + u + 1)
                            for j in range(JC // 2):
                                mm = nc.tensor.transpose(tp[0][:, j * P:(j + 1) * P],
                                                         prob[u % PB][:, j * P:(j + 1) * P], ident)
                            mm.then_inc(s["tp_lo"], 1)
                            pe.wait_ge(s["ev_hi"], u0 + u + 2)
                            for j in range(JC // 2):
                                mm = nc.tensor.transpose(tp[1][:, j * P:(j + 1) * P],
                                                         prob[u % PB][:, 512 + j * P:512 + (j + 1) * P], ident)
                            mm.then_inc(s["tp_hi"], 1)

                        def values(h):
                            pe.wait_ge(s["ev_lo"], u0 + (h + 1) * TB + 1)
                            pe.wait_ge(s["ev_hi"], u0 + (h + 1) * TB + 2)
                            rows = slice((h % 2) * HD, (h % 2 + 1) * HD)
                            for j in range(JC):
                                mm = nc.tensor.matmul(av[h // 2][rows, :], v[:, j, h * HD:(h + 1) * HD], prob_t[:, j, :],
                                                      start=(j == 0), stop=(j == JC - 1))
                            mm.then_inc(s["av_done"], 1)

                        for u in range(UB + 2):
                            if u < UB:
                                scores(u)
                            if u >= 2:
                                turn(u - 2)
                            if u >= 2 and (u - 2) % TB == TB - 1:
                                values((u - 2) // TB)
                        pe.wait_ge(s["att_ready"], b * KD + 2 * KD)
                        for t in range(TB):
                            for k in range(KD):
                                mm = nc.tensor.matmul(proj[:, t * D:(t + 1) * D], att_t[:, k, t * P:(t + 1) * P], wo[:, k, :],
                                                      start=(k == 0), stop=(k == KD - 1))
                            if t % 2:
                                mm.then_inc(s["proj_done"], 1)

            @block.scalar
            def _(act):
                act.sem_inc(s["exp_done"], 2)
                act.sem_inc(s["ev_lo"], 1)
                act.sem_inc(s["att_ready"], 2)
                with act.Fori(0, B // 2) as pair:
                    for q in range(2):
                        b = pair * 2 + q
                        u0 = pair * (2 * UB) + q * UB
                        act.wait_ge(s["xn_tp"], b * KD + 1)
                        nc.scalar.activation(xn_t[:, 0, :], av[0][:], ACT.Copy).then_inc(s["xn_ev_a"], 1)
                        act.wait_ge(s["kv_done"], b * 4 + 1)
                        nc.scalar.activation(k_t[:, 0, :], sc[0][:], ACT.Copy).then_inc(s["k_ready"], 1)
                        for c in range(KD):
                            act.wait_ge(s["q_done"], b * KD + c + 1)
                            nc.scalar.activation(q_t[:, c, :], av[c][:], ACT.Copy,
                                                 scale=float(HD) ** -0.5).then_inc(s["q_ready"], 1)
                        act.wait_ge(s["kv_done"], b * 4 + 3)
                        nc.scalar.activation(v[:, 0:JC // 2, :], sc[0][:].rearrange("p (j d) -> p j d", d=D),
                                             ACT.Copy).then_inc(s["v_a"], 1)
                        for u in range(UB + 2):
                            if u < UB:
                                w = u % PB
                                act.wait_ge(s["nmax_ready"], u0 + u + 1)
                                nc.scalar.activation(prob[w][:], prob[w][:], ACT.Exp, bias=nmax[:, w:w + 1],
                                                     accum_out=rsum[:, w:w + 1]).then_inc(s["exp_done"], 1)
                            if u >= 2:
                                t = (u - 2) % TB
                                act.wait_ge(s["tp_lo"], u0 + u - 1)
                                nc.scalar.activation(prob_t[:, 0:JC // 2, t * P:(t + 1) * P],
                                                     tp[0][:].rearrange("p (j i) -> p j i", i=P), ACT.Copy).then_inc(s["ev_lo"], 1)
                            if u == UB // 2 + 3:
                                act.wait_ge(s["av_done"], b * H + 2)
                                nc.scalar.activation(att_t[:, 0, :], av[0][:], ACT.Copy).then_inc(s["att_ready"], 1)
                        act.wait_ge(s["av_done"], b * H + 4)
                        nc.scalar.activation(att_t[:, 1, :], av[1][:], ACT.Copy).then_inc(s["att_ready"], 1)

            @block.vector
            def _(dve):
                dve.sem_inc(s["ev_hi"], 2)
                dve.sem_inc(s["x_ready"], 2)
                with dve.Fori(0, B // 2) as pair:
                    for q in range(2):
                        b, g0 = pair * 2 + q, pair * (2 * TB) + q * TB
                        u0 = pair * (2 * UB) + q * UB
                        for t in range(TB):
                            normalise(nc, m, xn[q][:, t, :], g0 + t).then_inc(s["xn_ready"], 1)
                        dve.wait_ge(s["xn_tp"], b * KD + 2)
                        nc.vector.tensor_copy(xn_t[:, 1, :], av[1][:]).then_inc(s["xn_ev_d"], 1)
                        dve.wait_ge(s["kv_done"], b * 4 + 2)
                        nc.vector.tensor_copy(k_t[:, 1, :], sc[1][:]).then_inc(s["k_ready"], 1)
                        dve.wait_ge(s["kv_done"], b * 4 + 4)
                        nc.vector.tensor_copy(v[:, JC // 2:JC, :], sc[1][:].rearrange("p (j d) -> p j d", d=D)).then_inc(s["v_d"], 1)
                        dve.wait_ge(s["minf_ready"], b + 2)

                        def maximum(u):
                            t, w = u % TB, u % PB
                            dve.wait_ge(s["qk_done"], u0 + u + 1)
                            if u >= PB - 2:
                                dve.wait_ge(s["ev_hi"], u0 + u + 3 - PB)
                            apart(m, dve)
                            nc.vector.tensor_tensor_reduce(out=prob[w][:], in0=sc[u % 2][:], in1=minf[:, t, :], scale=1.0,
                                                           scalar=-BIG, op0=ALU.add, op1=ALU.max,
                                                           accum_out=max_[:, w:w + 1]).then_inc(s["max_done"], 1)
                            dve.wait_ge(s["max_done"], u0 + u + 1)
                            nc.vector.tensor_scalar(nmax[:, w:w + 1], max_[:, w:w + 1], -1.0, None, ALU.mult).then_inc(s["nmax_ready"], 1)

                        def scale(u):
                            w = u % PB
                            dve.wait_ge(s["exp_done"], u0 + u + 3)
                            nc.vector.reciprocal(rinv[:, w:w + 1], rsum[:, w:w + 1]).then_inc(s["inv_done"], 1)
                            dve.wait_ge(s["inv_done"], u0 + u + 1)
                            nc.vector.tensor_scalar(prob[w][:], prob[w][:], rinv[:, w:w + 1], None, ALU.mult).then_inc(s["prob_ready"], 1)

                        def evict(u):
                            t = u % TB
                            dve.wait_ge(s["tp_hi"], u0 + u + 1)
                            nc.vector.tensor_copy(prob_t[:, JC // 2:JC, t * P:(t + 1) * P],
                                                  tp[1][:].rearrange("p (j i) -> p j i", i=P)).then_inc(s["ev_hi"], 1)

                        for u in range(UB + 2):
                            if u < UB:
                                maximum(u)
                            if 1 <= u <= UB:
                                scale(u - 1)
                            if u >= 2:
                                evict(u - 2)
                        for half in range(2):
                            dve.wait_ge(s["proj_done"], b * 2 + half + 1)
                            xs = m.x[:, ds(g0 + 2 * half, 2), :]
                            nc.vector.tensor_tensor(xs, xs, proj[:, half * 2 * D:(half + 1) * 2 * D]
                                                    .rearrange("p (t d) -> p t d", d=D), ALU.add).then_inc(s["x_ready"], 1)


def experts(nc, m, dram, layer):
    first = layer == 0
    ne = 12 if first else E
    F = 512 if first else 1024
    FC = F // P
    w1, w2 = (m.w1_0, m.w2_0) if first else (m.w1_1, m.w2_1)
    tag = "b_" if first else "d_"
    with ExitStack() as ctx:
        sem = lambda n: nc.alloc_semaphore(name=n)
        sb = lambda n, s, d=F32: ctx.enter_context(nc.sbuf_tensor(tag + n, s, d))
        ps = lambda n, s: ctx.enter_context(nc.psum_tensor(tag + n, s, F32))
        ident = m.const[:, C_IDENT:C_IDENT + P]
        ones = m.const[:, C_ONES:C_ONES + P]
        before = m.const[:, C_BEFORE:C_BEFORE + P]

        gate_slot = sb("gate_slot", [P, NBX])
        row_slot = sb("row_slot", [P, NBX], I32)
        expert_of = sb("expert_of", [1, NBX], I32)
        if not first:
            b1 = sb("b1", [P, E, FC])
            b2 = sb("b2", [P, E, D])
            ln_w = sb("ln_w", [P, E, KD])
            ln_b = sb("ln_b", [P, E, KD])
        scratch = ExitStack()
        sr = lambda n, s, d=F32: scratch.enter_context(nc.sbuf_tensor(tag + n, s, d))
        xn = [sr(f"xn{q}", [P, D]) for q in range(2)]
        xn_t = [sr(f"xn_t{q}", [P, KD, P]) for q in range(2)]
        gw = sr("gw", [P, KD, ne])
        ebias = sr("ebias", [P, ne])
        logit = sr("logit", [P, ne, T])
        logit2 = sr("logit2", [P, ne, T])
        grid = sr("grid", [P, ne, T])
        pick = [sr(f"pick{k}", [P, ne, T]) for k in range(2)]
        top = [sr(f"top{k}", [P, T]) for k in range(2)]
        idx = [sr(f"idx{k}", [P, T]) for k in range(2)]
        g = [sr(f"g{k}", [P, T]) for k in range(2)]
        zero = [sr(f"zero{k}", [P, T]) for k in range(2)]
        dlog = sr("dlog", [P, T])
        e2 = sr("e2", [P, T])
        den = sr("den", [P, T])
        wz = sr("wz", [P, T])
        load = sr("load", [P, E, T])
        tot = sr("tot", [P, E, T])
        cum = sr("cum", [P, E, T])
        place = sr("place", [P, E, T])
        count = sr("count", [P, E])
        nblk = sr("nblk", [P, E])
        endb = sr("endb", [P, E])
        shift = sr("shift", [P, E])
        pos = [sr(f"pos{k}", [P, T]) for k in range(2)]
        pos_i = [sr(f"pos_i{k}", [P, T], I32) for k in range(2)]
        lane_i = [sr(f"lane_i{k}", [P, T], I32) for k in range(2)]
        lane = [sr(f"lane{k}", [P, T]) for k in range(2)]
        blk_i = [sr(f"blk_i{k}", [P, T], I32) for k in range(2)]
        blk = [sr(f"blk{k}", [P, T]) for k in range(2)]
        in_blk = sr("in_blk", [P, T, NBX])
        val = [sr(f"val{k}", [P, T, 2, NBX]) for k in range(2)]
        in_lane = sr("in_lane", [P, T, P])
        empty = sr("empty", [P, NBX])
        rowf = sr("rowf", [P, NBX])
        bcmp = sr("bcmp", [1, NBX, E])
        bsumf = sr("bsumf", [1, NBX])
        bminf = sr("bminf", [1, NBX])
        alpha = sr("alpha", [P, E])
        xn_all = sr("xn_all", [P, T, D])
        scratch.close()
        xg = [sb(f"xg{q}", [P, D]) for q in range(LANES)]
        rows = [sb(f"rows{q}", [P, 1], I32) for q in range(LANES)]
        add_rows = [sb(f"add_rows{q}", [P, 1], I32) for q in range(LANES)]
        y = [sb(f"y{q}", [P, D]) for q in range(LANES)]
        yb = sb("yb", [P, D])
        xg_t = sb("xg_t", [P, KD, P])
        hid = sb("hid", [P, F])
        hid_t = sb("hid_t", [P, FC, P])

        tpx = [ps(f"tpx{q}", [P, 512]) for q in range(2)]
        hps = ps("hps", [P, 1024])
        hps_t = [ps(f"hps_t{q}", [P, 512]) for q in range(2)]
        yps = ps("yps", [P, 512])
        lps = [yps, ps("mps", [P, 512])]

        names = ("w_in xn_ready xn_tp xn_t_ready logit_done logit_ready xn_kept step tot_ready exp_ready "
                 "lane_ready val_ready lane_used map_done route_ready xn_out "
                 "bias_in rows_ready add_rows_ready xg_tp xg_t_ready up_done hid_ready hid_tp_lo hid_tp_hi "
                 "hid_t_ready down_done yb_ready y_ready y_free added out_done").split()
        s = {n: sem(tag + n) for n in names}
        gathered = [sem(f"{tag}gathered{q}") for q in range(LANES)]

        with nc.Block() as block:
            @block.sync
            def _(sp):
                sp.dma_start(gw[:], dram["gate_0" if first else "gate_1"].rearrange("(k p) e -> p k e", p=P)).then_inc(s["w_in"], 16)
                if first:
                    sp.dma_start(ebias[:], dram["ebias"].partition_broadcast(P)).then_inc(s["w_in"], 16)
                else:
                    sp.dma_start(alpha[:], dram["alpha"].partition_broadcast(P)).then_inc(s["w_in"], 16)
                    sp.dma_start(b1[:], dram["b1"]).then_inc(s["bias_in"], 16)
                    sp.dma_start(b2[:], dram["b2"].partition_broadcast(P)).then_inc(s["bias_in"], 16)
                    sp.dma_start(ln_w[:], dram["ln_w"]).then_inc(s["bias_in"], 16)
                    sp.dma_start(ln_b[:], dram["ln_b"]).then_inc(s["bias_in"], 16)
                    for e in range(E):
                        sp.dma_start(w1[:, e, :, :], dram["w1_1"][e].rearrange("(k p) f -> p k f", p=P)).then_inc(m.s_w1, 16)
                sp.wait_ge(s["xn_kept"], T + 2)
                sp.dma_start(dram["rows"][0:T * P, :].rearrange("(t p) d -> p t d", p=P), xn_all[:]).then_inc(s["xn_out"], 16)
                sp.dma_start(dram["rows"][T * P:(T + 1) * P, :], xn_all[:, 0, :]).then_inc(s["xn_out"], 16)
                if first:
                    sp.wait_ge(s["route_ready"], 1)
                sp.dma_start(dram["acc"][0:T * P, :].rearrange("(t p) d -> p t d", p=P), m.x[:]).then_inc(s["xn_out"], 16)
                sp.dma_start(dram["acc"][T * P:(T + 1) * P, :], m.x[:, 0, :]).then_inc(s["xn_out"], 16)
                sp.wait_ge(s["xn_out"], 64)

            @block.tensor
            def _(pe):
                pe.wait_ge(s["w_in"], 32)
                with pe.Fori(0, T // 2) as i:
                    for q in range(2):
                        t = i * 2 + q
                        pe.wait_ge(s["xn_ready"], t + 1)
                        for k in range(KD):
                            mm = nc.tensor.transpose(tpx[q][:, k * P:(k + 1) * P], xn[q][:, k * P:(k + 1) * P], ident)
                        mm.then_inc(s["xn_tp"], 1)
                        pe.wait_ge(s["xn_t_ready"], t + 1)
                        pe.wait_ge(s["logit_ready"], t + 1)
                        for k in range(KD):
                            mm = nc.tensor.matmul(lps[q][:, 0:ne], xn_t[q][:, k, :], gw[:, k, :], start=(k == 0), stop=(k == KD - 1))
                        mm.then_inc(s["logit_done"], 1)
                pe.wait_ge(s["lane_ready"], 1)
                nc.tensor.matmul(yps[:, 0:E * T], before, load[:].rearrange("p e t -> p (e t)"), start=True, stop=True)
                nc.tensor.matmul(yps[:, E * T:2 * E * T], ones, load[:].rearrange("p e t -> p (e t)"),
                                 start=True, stop=True).then_inc(s["tot_ready"], 1)
                for k in range(2):
                    pe.wait_ge(s["lane_ready"], k + 2)
                    pe.wait_ge(s["val_ready"], k + 1)
                    for t in range(T):
                        mm = nc.tensor.matmul(hps[:, 0:2 * NBX], in_lane[:, t, :], val[k][:, t, :, :].rearrange("p a b -> p (a b)"),
                                              start=(k == 0 and t == 0), stop=(k == 1 and t == T - 1))
                    mm.then_inc(s["lane_used"], 1)

            @block.scalar
            def _(act):
                act.sem_inc(s["xn_kept"], 2)
                with act.Fori(0, T // 2) as i:
                    for q in range(2):
                        t = i * 2 + q
                        act.wait_ge(s["xn_tp"], t + 1)
                        nc.scalar.activation(xn_t[q][:], tpx[q][:, 0:D].rearrange("p (k t) -> p k t", k=KD),
                                             ACT.Copy).then_inc(s["xn_t_ready"], 1)
                        nc.scalar.activation(xn_all[:, ds(t, 1), :].rearrange("p a d -> p (a d)"), xn[q][:],
                                             ACT.Copy).then_inc(s["xn_kept"], 1)
                act.wait_ge(s["exp_ready"], 1)
                nc.scalar.activation(e2[:], dlog[:], ACT.Exp).then_inc(s["exp_ready"], 1)

            @block.vector
            def _(dve):
                dve.sem_inc(s["logit_ready"], 2)
                dve.wait_ge(s["w_in"], 32)
                with dve.Fori(0, T // 2) as i:
                    for q in range(2):
                        t = i * 2 + q
                        dve.wait_ge(s["xn_kept"], t + 1)
                        normalise(nc, m, xn[q][:], t).then_inc(s["xn_ready"], 1)
                    for q in range(2):
                        t = i * 2 + q
                        dve.wait_ge(s["logit_done"], t + 1)
                        out = logit[:, :, ds(t, 1)].rearrange("p e a -> p (e a)")
                        if first:
                            nc.vector.tensor_tensor(out, lps[q][:, 0:ne], ebias[:], ALU.add).then_inc(s["logit_ready"], 1)
                        else:
                            nc.vector.tensor_copy(out, lps[q][:, 0:ne]).then_inc(s["logit_ready"], 1)

                steps = [0]

                def after(ins):
                    steps[0] += 1
                    ins.then_inc(s["step"], 1)
                    dve.wait_ge(s["step"], steps[0])

                dve.wait_ge(s["logit_ready"], T + 2)
                V = nc.vector
                expert_no = m.const[:, C_EXP:C_EXP + ne * T].rearrange("p (e t) -> p e t", t=T)
                over_e = lambda a: a.rearrange("p e t -> p t e")
                by_e = lambda a, n=ne: a.unsqueeze(1).broadcast_to([P, n, T])
                by_t = lambda a: a.unsqueeze(2).broadcast_to([P, E, T])
                src = logit
                for k in range(2):
                    after(V.tensor_reduce(top[k][:], over_e(src[:]), AX.X, ALU.max))
                    after(V.tensor_tensor(grid[:], src[:], by_e(top[k][:]), ALU.is_equal))
                    after(V.scalar_tensor_tensor(grid[:].rearrange("p e t -> p (e t)"), grid[:].rearrange("p e t -> p (e t)"), -100.0,
                                                 m.const[:, C_EXP:C_EXP + ne * T], ALU.mult, ALU.add))
                    after(V.tensor_reduce(idx[k][:], over_e(grid[:]), AX.X, ALU.min))
                    after(V.tensor_scalar(idx[k][:], idx[k][:], 100.0, None, ALU.add))
                    after(V.tensor_tensor(pick[k][:], expert_no, by_e(idx[k][:]), ALU.is_equal))
                    if k == 0:
                        after(V.scalar_tensor_tensor(logit2[:], pick[0][:], -BIG, logit[:], ALU.mult, ALU.add))
                        src = logit2
                V.tensor_tensor(dlog[:], top[1][:], top[0][:], ALU.subtract).then_inc(s["exp_ready"], 1)
                V.tensor_tensor(load[:], pick[0][:, 0:E, :], pick[1][:, 0:E, :], ALU.add).then_inc(s["lane_ready"], 1)
                dve.wait_ge(s["exp_ready"], 2)
                after(V.tensor_scalar(den[:], e2[:], 1.0, None, ALU.add))
                after(V.reciprocal(g[0][:], den[:]))
                after(V.tensor_tensor(g[1][:], e2[:], g[0][:], ALU.mult))
                if first:
                    for k in range(2):
                        after(V.tensor_scalar(zero[k][:], idx[k][:], E - 0.5, None, ALU.is_gt))
                    after(V.tensor_tensor(wz[:], g[0][:], zero[0][:], ALU.mult))
                    after(V.tensor_tensor(den[:], g[1][:], zero[1][:], ALU.mult))
                    after(V.tensor_tensor(wz[:], wz[:], den[:], ALU.add))
                else:
                    for k in range(2):
                        after(V.tensor_tensor(grid[:], pick[k][:], by_t(alpha[:]), ALU.mult))
                        after(V.tensor_reduce(den[:], over_e(grid[:]), AX.X, ALU.add))
                        after(V.tensor_tensor(g[k][:], g[k][:], den[:], ALU.mult))
                dve.wait_ge(s["tot_ready"], 1)
                flat = lambda a: a.rearrange("p e t -> p (e t)")
                after(V.tensor_copy(flat(tot[:]), yps[:, E * T:2 * E * T]))
                after(V.tensor_tensor_scan(flat(cum[:]), m.const[:, C_ONES:C_ONES + E * T], flat(tot[:]), 0.0, ALU.mult, ALU.add))
                after(V.tensor_reduce(count[:], tot[:], AX.X, ALU.add))
                thr = m.const[:, C_THR:C_THR + T].unsqueeze(1).broadcast_to([P, E, T])
                after(V.tensor_tensor(place[:], by_t(count[:]), thr, ALU.is_gt))
                after(V.tensor_reduce(nblk[:], place[:], AX.X, ALU.add))
                after(V.tensor_tensor_scan(endb[:], m.const[:, C_ONES:C_ONES + E], nblk[:], 0.0, ALU.mult, ALU.add))
                after(V.tensor_tensor(shift[:], endb[:], nblk[:], ALU.subtract))
                after(V.scalar_tensor_tensor(shift[:], shift[:], float(P), count[:], ALU.mult, ALU.add))
                after(V.tensor_tensor(shift[:], shift[:], cum[:, :, T - 1], ALU.subtract))
                after(V.tensor_tensor(place[:], cum[:], tot[:], ALU.subtract))
                after(V.tensor_tensor(flat(place[:]), flat(place[:]), yps[:, 0:E * T], ALU.add))
                after(V.tensor_tensor(place[:], place[:], by_t(shift[:]), ALU.add))
                for k in range(2):
                    after(V.tensor_tensor(cum[:], pick[k][:, 0:E, :], place[:], ALU.mult))
                    after(V.tensor_reduce(pos[k][:], over_e(cum[:]), AX.X, ALU.add))
                    if first:
                        after(V.scalar_tensor_tensor(pos[k][:], zero[k][:], 64.0 * P, pos[k][:], ALU.mult, ALU.add))
                    after(V.tensor_copy(pos_i[k][:], pos[k][:]))
                    after(V.tensor_scalar(lane_i[k][:], pos_i[k][:], P - 1, None, ALU.bitwise_and))
                    after(V.tensor_scalar(blk_i[k][:], pos_i[k][:], 7, None, ALU.arith_shift_right))
                    after(V.tensor_copy(lane[k][:], lane_i[k][:]))
                    after(V.tensor_copy(blk[k][:], blk_i[k][:]))
                block_no = m.const[:, C_BLK:C_BLK + NBX].unsqueeze(1).broadcast_to([P, T, NBX])
                row_no = m.const[:, C_ROW:C_ROW + P].unsqueeze(1).broadcast_to([P, T, P])
                for k in range(2):
                    by_b = lambda a: a.unsqueeze(2).broadcast_to([P, T, NBX])
                    after(V.tensor_tensor(in_blk[:], block_no, by_b(blk[k][:]), ALU.is_equal))
                    after(V.tensor_tensor(val[k][:, :, 0, :], in_blk[:], by_b(m.const[:, C_TOKEN:C_TOKEN + T]), ALU.mult))
                    V.tensor_tensor(val[k][:, :, 1, :], in_blk[:], by_b(g[k][:]), ALU.mult).then_inc(s["val_ready"], 1)
                    dve.wait_ge(s["val_ready"], k + 1)
                    if k:
                        dve.wait_ge(s["lane_used"], k)
                    V.tensor_tensor(in_lane[:], row_no, lane[k][:].unsqueeze(2).broadcast_to([P, T, P]),
                                    ALU.is_equal).then_inc(s["lane_ready"], 1)
                after(V.tensor_tensor(bcmp[:], m.const[0:1, C_BLK:C_BLK + NBX].unsqueeze(2).broadcast_to([1, NBX, E]),
                                      endb[0:1, :].unsqueeze(1).broadcast_to([1, NBX, E]), ALU.is_ge))
                after(V.tensor_reduce(bsumf[:], bcmp[:], AX.X, ALU.add))
                after(V.tensor_scalar(bminf[:], bsumf[:], E - 1.0, None, ALU.min))
                after(V.tensor_copy(expert_of[:], bminf[:]))
                if first:
                    for t in range(T):
                        last = V.scalar_tensor_tensor(m.x[:, t, :], xn_all[:, t, :], wz[:, t:t + 1], m.x[:, t, :], ALU.mult, ALU.add)
                    after(last)
                dve.wait_ge(s["lane_used"], 2)
                after(V.tensor_copy(gate_slot[:], hps[:, NBX:2 * NBX]))
                after(V.tensor_scalar(empty[:], hps[:, 0:NBX], 0.0, None, ALU.is_equal))
                after(V.scalar_tensor_tensor(rowf[:], empty[:], m.const[:, C_PAD:C_PAD + 1], hps[:, 0:NBX], ALU.mult, ALU.add))
                after(V.tensor_scalar(rowf[:], rowf[:], -1.0, None, ALU.add))
                after(V.tensor_copy(row_slot[:], rowf[:]))
                dve.sem_inc(s["route_ready"], 1)

        with nc.Block() as block:
            @block.sync
            def _(sp):
                sp.wait_ge(s["added"], 16 * NB)
                src = dram["acc"][0:T * P, :]
                if first:
                    sp.dma_start(m.x[:], src.rearrange("(t p) d -> p t d", p=P)).then_inc(s["out_done"], 16)
                else:
                    sp.dma_start(dram["out"], src).then_inc(s["out_done"], 16)
                sp.wait_ge(s["out_done"], 16)

            @block.gpsimd
            def _(pool):
                def gather(n, q):
                    nc.gpsimd.tensor_copy(rows[q][:], row_slot[:, ds(n, 1)]).then_inc(s["rows_ready"], 1)
                    pool.wait_ge(s["rows_ready"], n + 1)
                    apart(m, pool)
                    nc.gpsimd.indirect_dma_start(out=xg[q][:], out_offset=None, in_=dram["rows"],
                                                 in_offset=bass.IndirectOffsetOnAxis(ap=rows[q][:], axis=0)).then_inc(gathered[q], 16)

                def add(n, q):
                    nc.gpsimd.tensor_copy(add_rows[q][:], row_slot[:, ds(n, 1)]).then_inc(s["add_rows_ready"], 1)
                    pool.wait_ge(s["add_rows_ready"], n + 1)
                    pool.wait_ge(s["y_ready"], n + 2)
                    if q:
                        pool.wait_ge(s["added"], n * 16)
                        pool.sem_inc(s["y_free"], 1)
                    else:
                        apart(m, pool)
                    nc.gpsimd.indirect_dma_start(out=dram["acc"], out_offset=bass.IndirectOffsetOnAxis(ap=add_rows[q][:], axis=0),
                                                 in_=y[q][:], in_offset=None, compute_op=ALU.add).then_inc(s["added"], 16)
                    if q == LANES - 1:
                        pool.wait_ge(s["added"], n * 16 + 16)
                        pool.sem_inc(s["y_free"], 1)

                for q in range(LANES):
                    gather(q, q)
                with pool.Fori(0, NB // LANES - 1) as i:
                    for q in range(LANES):
                        n = i * LANES + q
                        pool.wait_ge(s["xg_tp"], n + 1)
                        pool.wait_ge(gathered[q], i * 16 + 16)
                        gather(n + LANES, q)
                        add(n, q)
                for q in range(LANES):
                    add(NB - LANES + q, q)

            @block.tensor
            def _(pe):
                if first:
                    pe.wait_ge(m.s_w0, 16 * 2 * E)
                else:
                    pe.wait_ge(m.s_w1, 16 * E)
                    pe.wait_ge(m.s_w2, 16 * E)

                def expert(n):
                    return pe.value_load(expert_of[0:1, ds(n, 1)], min_val=0, max_val=E - 1)

                def turn_in(n, q, turn):
                    pe.wait_ge(gathered[q], turn * 16 + 16)
                    pe.wait_ge(s["xg_t_ready"], n + 1)
                    for k in range(KD):
                        mm = nc.tensor.transpose(tpx[0][:, k * P:(k + 1) * P], xg[q][:, k * P:(k + 1) * P], ident)
                    mm.then_inc(s["xg_tp"], 1)

                def up(n):
                    e = expert(n)
                    pe.wait_ge(s["xg_t_ready"], n + 2)
                    pe.wait_ge(s["hid_ready"], n + 1)
                    for c in range(F // 512):
                        for k in range(KD):
                            mm = nc.tensor.matmul(hps[:, c * 512:(c + 1) * 512], xg_t[:, k, :],
                                                  w1[:, ds(e, 1), k, c * 512:(c + 1) * 512].rearrange("p a f -> p (a f)"),
                                                  start=(k == 0), stop=(k == KD - 1))
                    mm.then_inc(s["up_done"], 1)

                def turn_hidden(n):
                    pe.wait_ge(s["hid_ready"], n + 2)
                    for half, done in enumerate(("hid_tp_lo", "hid_tp_hi")):
                        pe.wait_ge(s["hid_t_ready"], n * 2 + half + 1)
                        for c in range(FC // 2):
                            at = half * (FC // 2) + c
                            mm = nc.tensor.transpose(hps_t[half][:, c * P:(c + 1) * P], hid[:, at * P:(at + 1) * P], ident)
                        mm.then_inc(s[done], 1)

                def down(n):
                    e = expert(n)
                    pe.wait_ge(s["yb_ready" if not first else "y_ready"], n + 1)
                    for c in range(FC):
                        if c % (FC // 2) == 0:
                            pe.wait_ge(s["hid_t_ready"], n * 2 + c // (FC // 2) + 3)
                        mm = nc.tensor.matmul(yps[:, 0:D], hid_t[:, c, :], w2[:, ds(e, 1), c, :].rearrange("p a d -> p (a d)"),
                                              start=(c == 0), stop=(c == FC - 1))
                    mm.then_inc(s["down_done"], 1)

                turn_in(0, 0, 0)
                up(0)
                turn_in(1, 1, 0)
                with pe.Fori(0, NB // LANES - 1) as i:
                    for q in range(LANES):
                        n = i * LANES + q
                        turn_hidden(n)
                        up(n + 1)
                        turn_in(n + 2, (q + 2) % LANES, i + (q + 2) // LANES)
                        down(n)
                for q in range(LANES):
                    n = NB - LANES + q
                    turn_hidden(n)
                    if q + 1 < LANES:
                        up(n + 1)
                    if q + 2 < LANES:
                        turn_in(n + 2, q + 2, NB // LANES - 1)
                    down(n)

            @block.scalar
            def _(act):
                act.sem_inc(s["hid_t_ready"], 2)
                if not first:
                    act.wait_ge(s["bias_in"], 64)
                with act.Fori(0, NB) as n:
                    if not first:
                        e = act.value_load(expert_of[0:1, ds(n, 1)], min_val=0, max_val=E - 1)
                    for half in range(2):
                        src = hps_t[half][:, 0:F // 2].rearrange("p (c t) -> p c t", t=P)
                        c0 = half * (FC // 2)
                        if half == 0:
                            act.wait_ge(s["hid_tp_lo"], n + 1)
                        else:
                            act.wait_ge(s["hid_tp_hi"], n + 2)
                        if first:
                            op = nc.scalar.activation(hid_t[:, c0:c0 + FC // 2, :], src, ACT.Silu)
                        else:
                            for c in range(FC // 2):
                                op = nc.scalar.activation(hid_t[:, c0 + c, :], src[:, c, :], ACT.Gelu_apprx_tanh,
                                                          bias=b1[:, ds(e, 1), c0 + c])
                        op.then_inc(s["hid_t_ready"], 1)

            @block.vector
            def _(dve):
                for credit in ("xg_t_ready", "hid_ready", "hid_tp_hi", "yb_ready", "y_ready"):
                    dve.sem_inc(s[credit], 1)
                dve.sem_inc(s["y_free"], LANES)
                if not first:
                    dve.wait_ge(s["bias_in"], 64)

                def expert(n):
                    return None if first else dve.value_load(expert_of[0:1, ds(n, 1)], min_val=0, max_val=E - 1)

                def take_in(n):
                    e = expert(n)
                    dve.wait_ge(s["xg_tp"], n + 1)
                    if first:
                        nc.vector.tensor_copy(xg_t[:], tpx[0][:, 0:D].rearrange("p (k t) -> p k t", k=KD)).then_inc(s["xg_t_ready"], 1)
                    else:
                        for k in range(KD):
                            op = nc.vector.tensor_scalar(xg_t[:, k, :], tpx[0][:, k * P:(k + 1) * P],
                                                         ln_w[:, ds(e, 1), k], ln_b[:, ds(e, 1), k], ALU.mult, ALU.add)
                        op.then_inc(s["xg_t_ready"], 1)

                def take_hidden(n):
                    dve.wait_ge(s["up_done"], n + 1)
                    dve.wait_ge(s["hid_tp_hi"], n + 1)
                    nc.vector.tensor_copy(hid[:], hps[:, 0:F]).then_inc(s["hid_ready"], 1)

                def result(n, q):
                    e = expert(n)
                    dve.wait_ge(s["down_done"], n + 1)
                    dve.wait_ge(s["y_free"], n + 1)
                    gate = gate_slot[:, ds(n, 1)]
                    if first:
                        nc.vector.tensor_scalar(y[q][:], yps[:, 0:D], gate, None, ALU.mult).then_inc(s["y_ready"], 1)
                    else:
                        dve.wait_ge(s["y_ready"], n + 1)
                        nc.vector.tensor_tensor(yb[:], yps[:, 0:D], b2[:, ds(e, 1), :].rearrange("p a d -> p (a d)"),
                                                ALU.add).then_inc(s["yb_ready"], 1)
                        dve.wait_ge(s["yb_ready"], n + 2)
                        nc.vector.tensor_scalar(y[q][:], yb[:], gate, None, ALU.mult).then_inc(s["y_ready"], 1)

                take_in(0)
                take_hidden(0)
                take_in(1)
                with dve.Fori(0, NB // LANES - 1) as i:
                    for q in range(LANES):
                        n = i * LANES + q
                        take_hidden(n + 1)
                        take_in(n + 2)
                        result(n, q)
                for q in range(LANES):
                    n = NB - LANES + q
                    if q + 1 < LANES:
                        take_hidden(n + 1)
                    if q + 2 < LANES:
                        take_in(n + 2)
                    result(n, q)


def build(nc, dram):
    m = Mem()
    with ExitStack() as top:
        m.sem = lambda name: top.enter_context(nc.semaphore(name))
        sb = lambda n, s, d=F32: top.enter_context(nc.sbuf_tensor(n, s, d))
        m.x = sb("x", [P, T, D])
        m.const = sb("const", [P, C_END])
        m.bn = sb("bn", [P, T, 6])
        m.mean2, m.diff, m.m2, m.mean, m.dd, m.var, m.std, m.rstd = (
            sb(n, [P, T]) for n in "mean2 diff m2 mean dd var std rstd".split())
        m.nc = nc
        m.s_apart = [m.sem("apart_pool"), m.sem("apart_dve")]
        m.s_const = m.sem("const_in")
        m.s_w0 = m.sem("w0_in")
        m.s_w1 = m.sem("w1_in")
        m.s_w2 = m.sem("w2_in")
        load_phase(nc, m, dram)
        with ExitStack() as weights:
            m.w1_0 = weights.enter_context(nc.sbuf_tensor("w1_0", [P, E, KD, 512], F32))
            m.w2_0 = weights.enter_context(nc.sbuf_tensor("w2_0", [P, E, 4, D], F32))
            layer_norm_stats(nc, m, "n0")
            with nc.cleanup_on_exit():
                attention0(nc, m, dram)
            layer_norm_stats(nc, m, "n1")
            with nc.cleanup_on_exit():
                experts(nc, m, dram, 0)
        with ExitStack() as weights:
            m.w2_1 = weights.enter_context(nc.sbuf_tensor("w2_1", [P, E, 8, D], F32))
            layer_norm_stats(nc, m, "n2")
            with nc.cleanup_on_exit():
                attention1(nc, m, dram)
            layer_norm_stats(nc, m, "n3")
            m.w1_1 = weights.enter_context(nc.sbuf_tensor("w1_1", [P, E, KD, 1024], F32))
            with nc.cleanup_on_exit():
                experts(nc, m, dram, 1)


def kernel(x, ctx_1024, mask_BxSxS2_bf1, L0_xattn_w_sim, L0_xattn_b_sim, L0_xattn_W_qv, L0_xattn_b_qv,
           L0_ffn_gate_w, L0_ffn_expert_bias, L0_ffn_w1, L0_ffn_w2, L1_xattn_Wq, L1_xattn_Wkv, L1_xattn_Wo,
           L1_ffn_Wg, L1_ffn_alpha, L1_ffn_ln_w, L1_ffn_ln_b, L1_ffn_fc1_w, L1_ffn_fc1_b, L1_ffn_fc2_w, L1_ffn_fc2_b):
    import concourse.bacc as bacc
    from concourse.bass_utils import run_bass_kernel_spmd

    arr = lambda a: np.ascontiguousarray(np.asarray(a))
    ctx = arr(ctx_1024).reshape(B * M, D)
    host = {
        "x": arr(x).reshape(B * S, D),
        "const": shape_constants(),
        "ctx": ctx,
        "ctx_t": arr(ctx.T),
        "mask": arr(mask_BxSxS2_bf1).reshape(B * S, M).view(np.uint8),
        "w_sim": arr(arr(L0_xattn_w_sim).reshape(3 * KD, P).T),
        "b_sim": arr(L0_xattn_b_sim),
        "W_qv": arr(L0_xattn_W_qv),
        "b_qv": arr(L0_xattn_b_qv),
        "gate_0": arr(arr(L0_ffn_gate_w).T),
        "ebias": arr(L0_ffn_expert_bias),
        "w1_0": arr(arr(L0_ffn_w1).transpose(0, 2, 1)),
        "w2_0": arr(arr(L0_ffn_w2).transpose(0, 2, 1)),
        "Wq": arr(L1_xattn_Wq),
        "Wkv": arr(L1_xattn_Wkv),
        "Wo": arr(L1_xattn_Wo),
        "gate_1": arr(L1_ffn_Wg),
        "alpha": arr(L1_ffn_alpha),
        "ln_w": arr(arr(L1_ffn_ln_w).reshape(E, KD, P).transpose(2, 0, 1)),
        "ln_b": arr(arr(L1_ffn_ln_b).reshape(E, KD, P).transpose(2, 0, 1)),
        "w1_1": arr(L1_ffn_fc1_w),
        "b1": arr(arr(L1_ffn_fc1_b).reshape(E, -1, P).transpose(2, 0, 1)),
        "w2_1": arr(L1_ffn_fc2_w),
        "b2": arr(L1_ffn_fc2_b),
    }
    nc = bacc.Bacc("TRN2", target_bir_lowering=False, num_devices=1)
    dram = {n: nc.dram_tensor(f"in_{n}", a.shape, mybir.dt.from_np(a.dtype), kind="ExternalInput").ap()
            for n, a in host.items()}
    dram["rows"] = nc.dram_tensor("rows", [(T + 1) * P, D], F32, kind="Internal").ap()
    dram["acc"] = nc.dram_tensor("acc", [(T + 1) * P, D], F32, kind="Internal").ap()
    dram["out"] = nc.dram_tensor("out_x", [B * S, D], F32, kind="ExternalOutput").ap()
    build(nc, dram)
    r = run_bass_kernel_spmd(nc, [{f"in_{n}": a for n, a in host.items()}], core_ids=[0])
    return r.results[0]["out_x"].reshape(B, S, D)
```

```python
from contextlib import ExitStack

import numpy as np

import concourse.bass as bass
from concourse import mybir

F32 = mybir.dt.float32
BF16 = mybir.dt.bfloat16
F32R = mybir.dt.float32r
I32 = mybir.dt.int32
U8 = mybir.dt.uint8
ALU = mybir.AluOpType
ACT = mybir.ActivationFunctionType
AX = mybir.AxisListType
ds = bass.ds

P = 128
B, S, D = 4, 512, 256
M = 1024
T = B * S // P
TB = S // P
KD = D // P
JC = M // P
H, HD = 4, 64
SCALE = float(HD) ** -0.5
E = 8
NB = (2 * T * P - E) // P + E
NBX = NB + 1
EPS = 1e-5
BIG = 3e38
LAG = 3
PB = LAG + 1
LANES = 3

C_IDENT = 0
C_ONES = C_IDENT + P
C_BEFORE = C_ONES + P
C_ROW = C_BEFORE + P
C_TOKEN = C_ROW + P
C_PAD = C_TOKEN + T
C_ZERO = C_PAD + 1
C_EPS = C_ZERO + 1
C_THR = C_EPS + 1
C_BLK = C_THR + T
C_EXP = C_BLK + NBX
C_END = C_EXP + 12 * T


def shape_constants():
    c = np.zeros((P, C_END), np.float32)
    p = np.arange(P)
    c[:, C_IDENT:C_IDENT + P] = np.eye(P)
    c[:, C_ONES:C_ONES + P] = 1
    c[:, C_BEFORE:C_BEFORE + P] = p[:, None] < p[None, :]
    c[:, C_ROW:C_ROW + P] = p[None, :]
    c[:, C_TOKEN:C_TOKEN + T] = p[:, None] + P * np.arange(T)[None, :] + 1
    c[:, C_PAD] = T * P + p + 1
    c[:, C_EPS] = EPS
    c[:, C_THR:C_THR + T] = P * np.arange(T)
    c[:, C_BLK:C_BLK + NBX] = np.arange(NBX)
    c[:, C_EXP:C_END] = np.repeat(np.arange(12), T)[None, :]
    return c


def apart(m, eng):
    eng.sem_inc(m.s_apart[eng is m.nc.vector], 1)


class Mem:
    pass


def load_phase(nc, m, dram):
    s_in = m.s_const
    with nc.Block() as block:
        @block.sync
        def _(sp):
            sp.dma_start(m.x[:], dram["x"].rearrange("(t p) d -> p t d", p=P)).then_inc(s_in, 16)
            sp.dma_start(m.const[:], dram["const"]).then_inc(s_in, 16)
            sp.wait_ge(s_in, 32)


def layer_norm_stats(nc, m, tag):
    with (nc.semaphore(f"{tag}_bn_done") as s_st, nc.semaphore(f"{tag}_stat_step") as s_v,
          nc.semaphore(f"{tag}_sqrt_done") as s_sq, nc.Block() as block):
        @block.vector
        def _(dve):
            for t in range(T):
                nc.vector.bn_stats(m.bn[:, t, :], m.x[:, t, :]).then_inc(s_st, 1)
            dve.wait_ge(s_st, T)
            mean_e, m2_e, mean_o, m2_o = (m.bn[:, :, k] for k in (1, 2, 4, 5))
            nc.vector.tensor_tensor(m.mean2[:], mean_e, mean_o, ALU.add).then_inc(s_v, 1)
            nc.vector.tensor_tensor(m.diff[:], mean_e, mean_o, ALU.subtract).then_inc(s_v, 1)
            nc.vector.tensor_tensor(m.m2[:], m2_e, m2_o, ALU.add).then_inc(s_v, 1)
            dve.wait_ge(s_v, 3)
            nc.vector.tensor_scalar(m.mean[:], m.mean2[:], 0.5, None, ALU.mult).then_inc(s_v, 1)
            nc.vector.scalar_tensor_tensor(m.dd[:], m.diff[:], 0.25, m.diff[:], ALU.mult, ALU.mult).then_inc(s_v, 1)
            dve.wait_ge(s_v, 5)
            nc.vector.scalar_tensor_tensor(m.var[:], m.m2[:], 1.0 / D, m.dd[:], ALU.mult, ALU.add).then_inc(s_v, 1)
            dve.wait_ge(s_sq, 1)
            nc.vector.reciprocal(m.rstd[:], m.std[:]).then_inc(s_v, 1)

        @block.scalar
        def _(act):
            act.wait_ge(s_v, 6)
            nc.scalar.activation(m.std[:], m.var[:], ACT.Sqrt, bias=m.const[:, C_EPS:C_EPS + 1]).then_inc(s_sq, 1)


def normalise(nc, m, out, g):
    return nc.vector.tensor_scalar(out, m.x[:, ds(g, 1), :].rearrange("p a d -> p (a d)"),
                                   m.mean[:, ds(g, 1)], m.rstd[:, ds(g, 1)], ALU.subtract, ALU.mult)


def attention0(nc, m, dram):
    with ExitStack() as ctx:
        sem = lambda n: nc.alloc_semaphore(name="a_" + n)
        sb = lambda n, s, d=F32: ctx.enter_context(nc.sbuf_tensor("a_" + n, s, d))
        ps = lambda n, s: ctx.enter_context(nc.psum_tensor("a_" + n, s, F32))
        enc = [sb(f"enc{q}", [P, TB, D]) for q in range(2)]
        u_hi, u_lo = ([sb(f"u_{p}{q}", [P, KD, S], F32R) for q in range(2)] for p in ("hi", "lo"))
        ct_hi, ct_lo = ([sb(f"ct_{p}{q}", [P, KD, M], F32R) for q in range(2)] for p in ("hi", "lo"))
        cn_hi, cn_lo = ([sb(f"cn_{p}{q}", [P, JC, D], F32R) for q in range(2)] for p in ("hi", "lo"))
        raw = sb("raw", [P, KD * M])
        prob = [sb(f"prob{q}", [P, M]) for q in range(2)]
        pt_hi, pt_lo = (sb(f"pt_{p}", [P, JC, S], F32R) for p in ("hi", "lo"))
        u_t = sb("u_t", [P, KD, S])
        enc_t = sb("enc_t", [P, KD, S])
        hq_t = sb("hq_t", [P, KD, S])
        prod_t = sb("prod_t", [P, KD, S])
        wqv = sb("wqv", [P, 4 * KD, D])
        wenc = sb("wenc", [P, KD, D])
        bqv = sb("bqv", [P, D])
        wsim = sb("wsim", [P, 3 * KD])
        bsim = sb("bsim", [P, 1])
        nmax = sb("nmax", [P, T])
        rsum = sb("rsum", [P, T])
        rinv = sb("rinv", [P, T])
        mtot = sb("mtot", [P, TB])
        mrow = sb("mrow", [P, 1])
        ngmax1 = sb("ngmax1", [1, 1])
        ngmax = sb("ngmax", [P, 1])
        bexp = sb("bexp", [P, TB])
        bsum = sb("bsum", [P, 1])
        binv = sb("binv", [P, 1])
        hc = sb("hc", [P, KD])

        sc = ps("sc", [P, M])
        tp = [ps(f"tp{q}", [P, S]) for q in range(2)]
        av = [ps(f"av{q}", [P, S]) for q in range(2)]
        ex = ps("ex", [P, 2 * 512])
        ident = m.const[:, C_IDENT:C_IDENT + P]
        ones = m.const[:, C_ONES:C_ONES + P]
        LAST = TB - 1

        names = ("w_in raw_in raw_hi raw_lo enc_ready enc_tp u_ready u_hi u_lo qk_done max_done exp_done inv_done "
                 "prob_ready tp_lo tp_hi pt_hi pt_lo av_done hq_a hq_d enc_tp2 enc_t_ready a_done mtot_ready mrow_ready "
                 "mrow_tp ngmax1_ready ngmax_bc ngmax_ready bexp_ready hc_done binv_ready hc_ready wenc_ready "
                 "prod_ready bias_added proj_done x_ready").split()
        s = {n: sem(n) for n in names}

        def run(eng, begin, step):
            begin()
            for t in range(TB):
                step(0, 0, t, False, True, True)
            with eng.Fori(0, (B - 2) // 2) as pair:
                for q in (1, 0):
                    for t in range(TB):
                        step(pair * 2 + 2 - q, q, t, True, True, True)
            for t in range(TB):
                step(B - 1, (B - 1) % 2, t, True, True, False)
            for t in range(TB):
                step(B, B % 2, t, True, False, False)

        with nc.Block() as block:
            @block.sync
            def _(sp):
                for n in range(2 * B):
                    b = n // 2
                    if n:
                        sp.wait_ge(s["raw_lo"], 2 * n)
                    if n % 2 == 0:
                        sp.dma_start(raw[:].rearrange("p (k j) -> p k j", k=KD), dram["ctx_t"][:, b * M:(b + 1) * M]
                                     .rearrange("(k p) j -> p k j", p=P)).then_inc(s["raw_in"], 16)
                    else:
                        sp.dma_start(raw[:].rearrange("p (j d) -> p j d", d=D), dram["ctx"][b * M:(b + 1) * M, :]
                                     .rearrange("(j p) d -> p j d", p=P)).then_inc(s["raw_in"], 16)
                    if n == 0:
                        sp.dma_start(wsim[:], dram["w_sim"]).then_inc(s["w_in"], 16)
                        sp.dma_start(bsim[:], dram["b_sim"].partition_broadcast(P)).then_inc(s["w_in"], 16)
                        sp.dma_start(wqv[:], dram["W_qv"].rearrange("(c p) d -> p c d", p=P)).then_inc(s["w_in"], 16)
                        sp.dma_start(bqv[:], dram["b_qv"].partition_broadcast(P)).then_inc(s["w_in"], 16)

            def parts_of(hi_lo, half):
                return hi_lo[:].rearrange("p a b -> p (a b)")[:, half * M:(half + 1) * M]

            @block.tensor
            def _(pe):
                def three_passes(pieces, out, first, last):
                    pairs = [p for ah, al, bh, bl in pieces for p in ((ah, bh), (ah, bl), (al, bh))]
                    for n, (lhs, rhs) in enumerate(pairs):
                        mm = nc.tensor.matmul(out, lhs, rhs, start=(first and n == 0), stop=(last and n == len(pairs) - 1))
                    return mm

                def turn_enc(q, done):
                    for k in range(KD):
                        for t in range(TB):
                            mm = nc.tensor.transpose(ex[:, k * 512 + t * P:k * 512 + (t + 1) * P],
                                                     enc[q][:, t, k * P:(k + 1) * P], ident)
                        mm.then_inc(s[done], 1)

                def scores(b, q, t):
                    if t == 0:
                        pe.wait_ge(s["u_lo"], b * KD + KD)
                        pe.wait_ge(s["raw_lo"], b * 4 + 2)
                    pe.wait_ge(s["exp_done"], b * TB + t + 1)
                    ts = slice(t * P, (t + 1) * P)
                    for half in range(2):
                        hs = slice(half * 512, (half + 1) * 512)
                        mm = three_passes([(u_hi[q][:, k, ts], u_lo[q][:, k, ts], ct_hi[q][:, k, hs], ct_lo[q][:, k, hs])
                                           for k in range(KD)], sc[:, hs], True, True)
                    mm.then_inc(s["qk_done"], 1)

                def turn(g, q):
                    pe.wait_ge(s["prob_ready"], g + 1)
                    for half, done in enumerate(("tp_lo", "tp_hi")):
                        pe.wait_ge(s["pt_lo"], g * 2 + half + 1)
                        for j in range(JC // 2):
                            at = half * 512 + j * P
                            mm = nc.tensor.transpose(tp[half][:, j * P:(j + 1) * P], prob[q][:, at:at + P], ident)
                        mm.then_inc(s[done], 1)

                def values(b, q, pair, part):
                    pe.wait_ge(s["pt_lo"], (b * TB + pair * 2 + 2) * 2 + 2)
                    if pair == 0 and part == 0:
                        pe.wait_ge(s["raw_lo"], b * 4 + 4)
                        pe.wait_ge(s["hq_a"], b + 1)
                        pe.wait_ge(s["hq_d"], b + 1)
                    ts = slice(pair * 2 * P, (pair + 1) * 2 * P)
                    js = range(part * (JC // 2), (part + 1) * (JC // 2))
                    for k in range(KD):
                        ks = slice(k * P, (k + 1) * P)
                        mm = three_passes([(cn_hi[q][:, j, ks], cn_lo[q][:, j, ks], pt_hi[:, j, ts], pt_lo[:, j, ts])
                                           for j in js], av[k][:, ts], part == 0, part == 1)
                    if pair and part:
                        mm.then_inc(s["av_done"], 1)

                def project(b):
                    pe.wait_ge(s["wenc_ready"], b + 1)
                    pe.wait_ge(s["prod_ready"], b + 1)
                    for t in range(TB):
                        ts = slice(t * P, (t + 1) * P)
                        parts = ([(hq_t[:, k, ts], wqv[:, KD + k, :]) for k in range(KD)]
                                 + [(enc_t[:, k, ts], wenc[:, k, :]) for k in range(KD)]
                                 + [(prod_t[:, k, ts], wqv[:, 2 * KD + k, :]) for k in range(KD)])
                        for n, (lhs, rhs) in enumerate(parts):
                            mm = nc.tensor.matmul(ex[:, t * D:(t + 1) * D], lhs, rhs, start=(n == 0), stop=(n == len(parts) - 1))
                        if t % 2:
                            mm.then_inc(s["proj_done"], 1)

                def step(b, q, t, before, now, nxt):
                    p = b - 1
                    if now:
                        scores(b, q, t)
                    if before and t == 1:
                        pe.wait_ge(s["enc_t_ready"], p * KD + KD)
                        for tile in range(TB):
                            for k in range(KD):
                                mm = nc.tensor.matmul(ex[:, tile:tile + 1], enc_t[:, k, tile * P:(tile + 1) * P],
                                                      wsim[:, k:k + 1], start=(k == 0), stop=(k == KD - 1))
                        mm.then_inc(s["a_done"], 1)
                    if before and t == 2:
                        pe.wait_ge(s["ngmax1_ready"], p + 1)
                        nc.tensor.matmul(ex[:, 136:137], m.const[0:1, C_ONES:C_ONES + P], ngmax1[:],
                                         start=True, stop=True).then_inc(s["ngmax_bc"], 1)
                    if (before if t == 0 else now):
                        turn(b * TB + t - 1, (t - 1) % 2)
                    if nxt and t == LAST:
                        pe.wait_ge(s["enc_ready"], b * TB + TB + TB)
                        if before:
                            pe.wait_ge(s["hc_ready"], p + 1)
                        turn_enc(1 - q, "enc_tp")
                    if t == LAST:
                        if now:
                            values(b, q, 0, 0)
                    elif before:
                        values(p, 1 - q, *((0, 1), (1, 0), (1, 1))[t])
                    if before and t == 0:
                        pe.wait_ge(s["x_ready"], p * 2 + 2)
                        pe.wait_ge(s["u_ready"], b * KD + KD if now else b * KD)
                        turn_enc(1 - q, "enc_tp2")
                    if before and t == 1:
                        pe.wait_ge(s["mrow_ready"], p + 1)
                        nc.tensor.transpose(ex[0:1, 8:8 + P], mrow[:], ident).then_inc(s["mrow_tp"], 1)
                    if before and t == 2:
                        pe.wait_ge(s["bexp_ready"], p + 1)
                        nc.tensor.matmul(ex[:, 137:138], ones, bsum[:], start=True, stop=True)
                        for k in range(KD):
                            for tile in range(TB):
                                mm = nc.tensor.matmul(ex[:, 138 + k:139 + k], enc[1 - q][:, tile, k * P:(k + 1) * P],
                                                      bexp[:, tile:tile + 1], start=(tile == 0), stop=(tile == TB - 1))
                        mm.then_inc(s["hc_done"], 1)
                    if before and t == LAST:
                        if nxt:
                            pe.wait_ge(s["u_ready"], b * KD + 2 * KD)
                        project(p)

                def begin():
                    pe.wait_ge(s["enc_ready"], TB)
                    turn_enc(0, "enc_tp")
                    pe.wait_ge(s["w_in"], 64)

                run(pe, begin, step)

            @block.scalar
            def _(act):
                act.sem_inc(s["exp_done"], 1)
                act.sem_inc(s["hq_a"], 1)

                def split_high(n, hi):
                    act.wait_ge(s["raw_in"], n * 16 + 16)
                    for half in range(2):
                        nc.scalar.activation(parts_of(hi, half), raw[:, half * M:(half + 1) * M], ACT.Copy).then_inc(s["raw_hi"], 1)

                def u_high(b, q):
                    for k in range(KD):
                        act.wait_ge(s["u_ready"], b * KD + k + 1)
                        nc.scalar.activation(u_hi[q][:, k, :], u_t[:, k, :], ACT.Copy).then_inc(s["u_hi"], 1)

                def step(b, q, t, before, now, nxt):
                    p, g = b - 1, b * TB + t
                    if before and t == LAST:
                        act.wait_ge(s["av_done"], p + 1)
                        nc.scalar.activation(hq_t[:, 0, :], av[0][:], ACT.Copy).then_inc(s["hq_a"], 1)
                    if (before if t == 0 else now):
                        tile = (t - 1) % TB
                        for half, done in enumerate(("tp_lo", "tp_hi")):
                            act.wait_ge(s[done], g)
                            nc.scalar.activation(pt_hi[:, half * 4:half * 4 + 4, tile * P:(tile + 1) * P],
                                                 tp[half][:].rearrange("p (j i) -> p j i", i=P), ACT.Copy).then_inc(s["pt_hi"], 1)
                    if now:
                        act.wait_ge(s["max_done"], g + 1)
                        nc.scalar.activation(prob[t % 2][:], sc[:], ACT.Exp, bias=nmax[:, ds(g, 1)],
                                             accum_out=rsum[:, ds(g, 1)]).then_inc(s["exp_done"], 1)
                    if before and t == 0:
                        for k in range(KD):
                            act.wait_ge(s["enc_tp2"], p * KD + k + 1)
                            nc.scalar.activation(enc_t[:, k, :], ex[:, k * 512:(k + 1) * 512], ACT.Copy).then_inc(s["enc_t_ready"], 1)
                    if now and t == 0:
                        split_high(2 * b + 1, cn_hi[q])
                    if before and t == 2:
                        act.wait_ge(s["ngmax_ready"], p + 1)
                        nc.scalar.activation(bexp[:], mtot[:], ACT.Exp, bias=ngmax[:],
                                             accum_out=bsum[:]).then_inc(s["bexp_ready"], 1)
                    if nxt and t == 1:
                        split_high(2 * b + 2, ct_hi[1 - q])
                    if nxt and t == LAST:
                        u_high(b + 1, 1 - q)

                def begin():
                    split_high(0, ct_hi[0])
                    u_high(0, 0)

                run(act, begin, step)

            @block.vector
            def _(dve):
                dve.sem_inc(s["pt_lo"], 2)
                dve.sem_inc(s["hq_d"], 1)
                dve.sem_inc(s["x_ready"], 2)

                def norm_enc(b, q):
                    for t in range(TB):
                        normalise(nc, m, enc[q][:, t, :], b * TB + t).then_inc(s["enc_ready"], 1)

                def make_u(b):
                    for k in range(KD):
                        dve.wait_ge(s["enc_tp"], b * KD + k + 1)
                        nc.vector.tensor_scalar(u_t[:, k, :], ex[:, k * 512:(k + 1) * 512], wsim[:, 2 * KD + k:2 * KD + k + 1],
                                                wsim[:, KD + k:KD + k + 1], ALU.mult, ALU.add).then_inc(s["u_ready"], 1)

                def u_low(b, q):
                    for k in range(KD):
                        dve.wait_ge(s["u_hi"], b * KD + k + 1)
                        nc.vector.tensor_tensor(u_lo[q][:, k, :], u_t[:, k, :], u_hi[q][:, k, :], ALU.subtract).then_inc(s["u_lo"], 1)

                def step(b, q, t, before, now, nxt):
                    p, g = b - 1, b * TB + t
                    if now:
                        dve.wait_ge(s["qk_done"], g + 1)
                        nc.vector.tensor_reduce(nmax[:, ds(g, 1)], sc[:], AX.X, ALU.max, negate=True).then_inc(s["max_done"], 1)
                    if before and t == 1:
                        dve.wait_ge(s["a_done"], p + 1)
                        nc.vector.scalar_tensor_tensor(mtot[:], ex[:, 0:TB], bsim[:, 0:1], nmax[:, ds(p * TB, TB)],
                                                       ALU.add, ALU.subtract).then_inc(s["mtot_ready"], 1)
                        dve.wait_ge(s["mtot_ready"], p + 1)
                        nc.vector.tensor_reduce(mrow[:], mtot[:], AX.X, ALU.max).then_inc(s["mrow_ready"], 1)
                    if before and t == 2:
                        dve.wait_ge(s["ngmax_bc"], p + 1)
                        nc.vector.tensor_copy(ngmax[:], ex[:, 136:137]).then_inc(s["ngmax_ready"], 1)
                    if (before if t == 0 else now):
                        tile = (t - 1) % TB
                        for half in range(2):
                            js = slice(half * 4, half * 4 + 4)
                            dve.wait_ge(s["pt_hi"], g * 2 + half - 1)
                            nc.vector.tensor_tensor(pt_lo[:, js, tile * P:(tile + 1) * P], tp[half][:].rearrange("p (j i) -> p j i", i=P),
                                                    pt_hi[:, js, tile * P:(tile + 1) * P], ALU.subtract).then_inc(s["pt_lo"], 1)
                    if now:
                        dve.wait_ge(s["exp_done"], g + 2)
                        nc.vector.reciprocal(rinv[:, ds(g, 1)], rsum[:, ds(g, 1)]).then_inc(s["inv_done"], 1)
                    if before and t == 1:
                        dve.wait_ge(s["mrow_tp"], p + 1)
                        nc.vector.tensor_reduce(ngmax1[:], ex[0:1, 8:8 + P], AX.X, ALU.max, negate=True).then_inc(s["ngmax1_ready"], 1)
                    if before and t == 2:
                        dve.wait_ge(s["av_done"], p + 1)
                        nc.vector.tensor_copy(hq_t[:, 1, :], av[1][:]).then_inc(s["hq_d"], 1)
                        dve.wait_ge(s["hc_done"], p + 1)
                        nc.vector.reciprocal(binv[:], ex[:, 137:138]).then_inc(s["binv_ready"], 1)
                        dve.wait_ge(s["binv_ready"], p + 1)
                        nc.vector.tensor_scalar(hc[:], ex[:, 138:138 + KD], binv[:], None, ALU.mult).then_inc(s["hc_ready"], 1)
                    if nxt and t == 2:
                        norm_enc(b + 1, 1 - q)
                    if before and t == 2:
                        dve.wait_ge(s["hc_ready"], p + 1)
                        for k in range(KD):
                            op = nc.vector.scalar_tensor_tensor(wenc[:, k, :], wqv[:, 3 * KD + k, :], hc[:, k:k + 1],
                                                                wqv[:, k, :], ALU.mult, ALU.add)
                        op.then_inc(s["wenc_ready"], 1)
                    if nxt and t == LAST:
                        make_u(b + 1)
                        u_low(b + 1, 1 - q)
                    if before and t == LAST:
                        dve.wait_ge(s["bias_added"], p + 1)
                        for half in range(2):
                            dve.wait_ge(s["proj_done"], 2 * p + half + 1)
                            xs = m.x[:, ds(p * TB + 2 * half, 2), :]
                            nc.vector.tensor_tensor(xs, xs, ex[:, half * 512:(half + 1) * 512].rearrange("p (t d) -> p t d", d=D),
                                                    ALU.add).then_inc(s["x_ready"], 1)

                def begin():
                    norm_enc(0, 0)
                    dve.wait_ge(s["w_in"], 64)
                    make_u(0)
                    u_low(0, 0)

                run(dve, begin, step)

            @block.gpsimd
            def _(pool):
                def split_low(n, hi, lo):
                    for half in range(2):
                        pool.wait_ge(s["raw_hi"], n * 2 + half + 1)
                        nc.gpsimd.tensor_tensor(parts_of(lo, half), raw[:, half * M:(half + 1) * M], parts_of(hi, half),
                                                ALU.subtract).then_inc(s["raw_lo"], 1)

                def step(b, q, t, before, now, nxt):
                    p, g = b - 1, b * TB + t
                    if before and t == LAST:
                        pool.wait_ge(s["hq_a"], p + 2)
                        pool.wait_ge(s["hq_d"], p + 2)
                        nc.gpsimd.tensor_tensor(prod_t[:], enc_t[:], hq_t[:], ALU.mult).then_inc(s["prod_ready"], 1)
                    if now:
                        pool.wait_ge(s["inv_done"], g + 1)
                        apart(m, pool)
                        nc.gpsimd.tensor_scalar(prob[t % 2][:], prob[t % 2][:], rinv[:, ds(g, 1)], 1.0,
                                                ALU.mult, ALU.mult).then_inc(s["prob_ready"], 1)
                    if now and t == 0:
                        split_low(2 * b + 1, cn_hi[q], cn_lo[q])
                    if nxt and t == 1:
                        split_low(2 * b + 2, ct_hi[1 - q], ct_lo[1 - q])
                    if now and t == 2:
                        pool.wait_ge(s["enc_ready"], b * TB + TB)
                        xs = m.x[:, ds(b * TB, TB), :]
                        nc.gpsimd.tensor_tensor(xs, xs, bqv[:].unsqueeze(1).broadcast_to([P, TB, D]), ALU.add).then_inc(s["bias_added"], 1)

                def begin():
                    pool.wait_ge(s["w_in"], 64)
                    split_low(0, ct_hi[0], ct_lo[0])

                run(pool, begin, step)


def attention1(nc, m, dram):
    with ExitStack() as ctx:
        sem = lambda n: nc.alloc_semaphore(name=n)
        sb = lambda n, s, d=F32: ctx.enter_context(nc.sbuf_tensor("c_" + n, s, d))
        ps = lambda n, s: ctx.enter_context(nc.psum_tensor("c_" + n, s, F32))
        xn = sb("xn", [P, TB, D])
        xn_hi, xn_lo = (sb(f"xn_{p}", [P, KD, S], F32R) for p in ("hi", "lo"))
        ctx_t = sb("ctx_t", [P, KD, M])
        ctx_hi, ctx_lo = (sb(f"ctx_{p}", [P, KD, M], F32R) for p in ("hi", "lo"))
        mask = sb("mask", [P, TB, M], U8)
        mfin = sb("mfin", [P, M], BF16)
        minf = sb("minf", [P, TB, M], BF16)
        q_hi, q_lo = (sb(f"q_{p}", [P, KD, S], F32R) for p in ("hi", "lo"))
        k_hi, k_lo = (sb(f"k_{p}", [P, KD, M], F32R) for p in ("hi", "lo"))
        v2 = sb("v2", [P, JC, H, 2 * HD], F32R)
        prob = [sb(f"prob{q}", [P, M]) for q in range(PB)]
        pt_hi, pt_lo = (sb(f"pt_{p}", [P, JC, S], F32R) for p in ("hi", "lo"))
        att_lo = sb("att_lo", [HD, S])
        att_t = sb("att_t", [P, KD, S])
        wq = sb("wq", [P, KD, D])
        wq_hi, wq_lo = (sb(f"wq_{p}", [P, KD, D], F32R) for p in ("hi", "lo"))
        wkv = sb("wkv", [P, KD, 2 * D])
        wkv_hi, wkv_lo = (sb(f"wkv_{p}", [P, KD, 2 * D], F32R) for p in ("hi", "lo"))
        wo = sb("wo", [P, KD, D])
        UB = H * TB
        nmax = sb("nmax", [P, PB])
        rsum = sb("rsum", [P, PB])
        rinv = sb("rinv", [P, PB])

        sc = [ps(f"sc{q}", [P, M]) for q in range(2)]
        tp = [ps(f"tp{q}", [P, S]) for q in range(2)]
        av = [ps(f"av{q}", [P, S]) for q in range(2)]
        ident = m.const[:, C_IDENT:C_IDENT + P]

        names = ("w_in w_hi w_lo ctx_in mask_in mfin_ready minf_ready ctx_hi ctx_lo xn_ready xn_tp xn_hi xn_lo "
                 "q_done q_hi q_lo k_done k_hi k_lo v_done v_hi v_lo qk_done max_done exp_done inv_done prob_ready "
                 "tp_lo tp_hi pt_hi pt_lo av_done att_half att_ready proj_done x_ready").split()
        s = {n: sem("c_" + n) for n in names}

        CTX_STEP, TURN_X = 10, (11, 15)
        NORM_STEP = 5

        def three(a_hi, a_lo, b_hi, b_lo):
            return (a_hi, b_hi), (a_hi, b_lo), (a_lo, b_hi)

        def value_part(u):
            done, part = divmod(u - LAG - 2, 2)
            return None if not 0 <= done < UB // 2 else (done // 2, done % 2, part)

        with nc.Block() as block:
            @block.sync
            def _(sp):
                sp.dma_start(wq[:], dram["Wq"].rearrange("(k p) d -> p k d", p=P)).then_inc(s["w_in"], 16)
                sp.dma_start(wkv[:], dram["Wkv"].rearrange("(k p) d -> p k d", p=P)).then_inc(s["w_in"], 16)
                sp.dma_start(wo[:], dram["Wo"].rearrange("(k p) d -> p k d", p=P)).then_inc(s["w_in"], 16)
                for b in range(B):
                    if b:
                        sp.wait_ge(s["ctx_lo"], KD * b)
                    sp.dma_start(ctx_t[:], dram["ctx_t"][:, b * M:(b + 1) * M]
                                 .rearrange("(k p) j -> p k j", p=P)).then_inc(s["ctx_in"], 16)
                    if b:
                        sp.wait_ge(s["mfin_ready"], TB * b)
                    sp.dma_start(mask[:], dram["mask"][b * S:(b + 1) * S, :]
                                 .rearrange("(t p) j -> p t j", p=P)).then_inc(s["mask_in"], 16)

            @block.gpsimd
            def _(pool):
                pool.sem_inc(s["minf_ready"], 1)

                def ctx_low(b, k):
                    pool.wait_ge(s["ctx_hi"], b * KD + k + 1)
                    nc.gpsimd.tensor_tensor(ctx_lo[:, k, :], ctx_t[:, k, :], ctx_hi[:, k, :], ALU.subtract).then_inc(s["ctx_lo"], 1)

                def mask_tile(b, t):
                    if t == 0:
                        pool.wait_ge(s["mask_in"], b * 16 + 16)
                    pool.wait_ge(s["minf_ready"], b * TB + t + 1)
                    apart(m, pool)
                    nc.gpsimd.tensor_scalar(mfin[:], mask[:, t, :], -1.0, BIG, ALU.add, ALU.mult).then_inc(s["mfin_ready"], 1)
                    pool.wait_ge(s["mfin_ready"], b * TB + t + 1)
                    apart(m, pool)
                    nc.gpsimd.tensor_scalar(minf[:, t, :], mfin[:], 10.0, 1.0, ALU.mult, ALU.mult).then_inc(s["minf_ready"], 1)

                def batch(b, more):
                    for u in range(UB):
                        w = u % PB
                        pool.wait_ge(s["inv_done"], b * UB + u + 1)
                        apart(m, pool)
                        nc.gpsimd.tensor_scalar(prob[w][:], prob[w][:], rinv[:, w:w + 1], 1.0,
                                                ALU.mult, ALU.mult).then_inc(s["prob_ready"], 1)
                        if more and u in (CTX_STEP, CTX_STEP + 2):
                            ctx_low(b + 1, (u - CTX_STEP) // 2)
                        if more and u >= UB - TB:
                            mask_tile(b + 1, u - (UB - TB))

                for k in range(KD):
                    ctx_low(0, k)
                for t in range(TB):
                    mask_tile(0, t)
                with pool.Fori(0, B - 1) as b:
                    batch(b, True)
                batch(B - 1, False)

            @block.tensor
            def _(pe):
                def three_passes(out, parts):
                    pairs = [p for part in parts for p in three(*part)]
                    for n, (lhs, rhs) in enumerate(pairs):
                        mm = nc.tensor.matmul(out, lhs, rhs, start=(n == 0), stop=(n == len(pairs) - 1))
                    return mm

                def turn_x(b, k):
                    for t in range(TB):
                        mm = nc.tensor.transpose(av[k][:, t * P:(t + 1) * P], xn[:, t, k * P:(k + 1) * P], ident)
                    mm.then_inc(s["xn_tp"], 1)

                def k_proj(b, c):
                    cs = slice(c * P, (c + 1) * P)
                    pe.wait_ge(s["ctx_lo"], b * KD + KD)
                    for half in range(2):
                        hs = slice(half * 512, (half + 1) * 512)
                        mm = three_passes(sc[c][:, hs], [(wkv_hi[:, k, cs], wkv_lo[:, k, cs], ctx_hi[:, k, hs], ctx_lo[:, k, hs])
                                                         for k in range(KD)])
                    mm.then_inc(s["k_done"], 1)

                def q_proj(b, c):
                    cs = slice(c * P, (c + 1) * P)
                    pe.wait_ge(s["xn_lo"], b * KD + KD)
                    if c:
                        pe.wait_ge(s["q_lo"], b * KD + c)
                    three_passes(av[0][:], [(wq_hi[:, k, cs], wq_lo[:, k, cs], xn_hi[:, k, :], xn_lo[:, k, :])
                                            for k in range(KD)]).then_inc(s["q_done"], 1)

                def v_proj(b, c):
                    if c < 2:
                        pe.wait_ge(s["pt_lo"], b * 2 * UB + 2)
                    else:
                        pe.wait_ge(s["v_lo"], b * 4 + c - 1)
                    for j in range(2):
                        js = slice((c * 2 + j) * P, (c * 2 + j + 1) * P)
                        mm = three_passes(tp[c % 2][:, j * D:(j + 1) * D],
                                          [(ctx_hi[:, k, js], ctx_lo[:, k, js], wkv_hi[:, k, D:2 * D], wkv_lo[:, k, D:2 * D])
                                           for k in range(KD)])
                    mm.then_inc(s["v_done"], 1)

                def scores(b, u):
                    h, t = divmod(u, TB)
                    rows = slice((h % 2) * HD, (h % 2 + 1) * HD)
                    ts = slice(t * P, (t + 1) * P)
                    if u < 2:
                        pe.wait_ge(s["k_lo"], b * KD + u + 1)
                        pe.wait_ge(s["q_lo"], b * KD + KD)
                    else:
                        pe.wait_ge(s["max_done"], b * UB + u - 1)
                    for half in range(2):
                        hs = slice(half * 512, (half + 1) * 512)
                        mm = three_passes(sc[u % 2][:, hs], [(q_hi[rows, h // 2, ts], q_lo[rows, h // 2, ts],
                                                              k_hi[rows, h // 2, hs], k_lo[rows, h // 2, hs])])
                    mm.then_inc(s["qk_done"], 1)

                def turn(b, u):
                    pe.wait_ge(s["prob_ready"], b * UB + u + 1)
                    if u == 0:
                        pe.wait_ge(s["v_lo"], b * 4 + 4)
                    for half, done in enumerate(("tp_lo", "tp_hi")):
                        pe.wait_ge(s["pt_lo"], b * 2 * UB + u * 2 + half + 1)
                        for j in range(JC // 2):
                            at = half * 512 + j * P
                            mm = nc.tensor.transpose(tp[half][:, j * P:(j + 1) * P], prob[u % PB][:, at:at + P], ident)
                        mm.then_inc(s[done], 1)

                def values(b, more, h, pair, part):
                    pe.wait_ge(s["pt_lo"], b * 2 * UB + (h * TB + pair * 2 + 2) * 2 + 2)
                    if pair == 0 and part == 0:
                        pe.wait_ge(s["att_ready"], b * H + max(h, 1))
                        pe.wait_ge(s["x_ready"], b * 2 + 2)
                        if more and h >= 2:
                            pe.wait_ge(s["xn_lo"], b * KD + KD + h - 1)
                    ts = slice(pair * 2 * P, (pair + 1) * 2 * P)
                    for j in range(JC):
                        mm = nc.tensor.matmul(av[h % 2][:, ts], v2[:, j, h, :], (pt_hi, pt_lo)[part][:, j, ts],
                                              start=(part == 0 and j == 0), stop=(part == 1 and j == JC - 1))
                    if pair and part:
                        mm.then_inc(s["av_done"], 1)

                def step(b, more, u):
                    if u < UB:
                        scores(b, u)
                    elif more and u < UB + KD:
                        pe.wait_ge(s["max_done"], b * UB + UB - 1 + u - UB)
                        k_proj(b + 1, u - UB)
                    if u < UB + LAG:
                        turn(b, u - LAG)
                    if value_part(u):
                        values(b, more, *value_part(u))
                    if more and u in TURN_X:
                        k = TURN_X.index(u)
                        pe.wait_ge(s["xn_ready"], b * TB + TB + TB)
                        pe.wait_ge(s["att_ready"], b * H + k + 2)
                        turn_x(b + 1, k)
                    if more and UB + LAG - 1 <= u < UB + LAG + 1:
                        c = u - (UB + LAG - 1)
                        if c == 0:
                            pe.wait_ge(s["att_ready"], b * H + 4)
                        q_proj(b + 1, c)

                def project(b):
                    pe.wait_ge(s["att_ready"], b * H + H + 1)
                    for t in range(TB):
                        for k in range(KD):
                            mm = nc.tensor.matmul(av[t // 2][:, (t % 2) * D:(t % 2 + 1) * D], att_t[:, k, t * P:(t + 1) * P],
                                                  wo[:, k, :], start=(k == 0), stop=(k == KD - 1))
                        if t % 2:
                            mm.then_inc(s["proj_done"], 1)

                def begin(b, before):
                    scores(b, 0)
                    v_proj(b, 0)
                    v_proj(b, 1)
                    scores(b, 1)
                    if before:
                        project(b - 1)
                    scores(b, 2)
                    v_proj(b, 2)
                    v_proj(b, 3)

                def batch(b, more):
                    for u in range(LAG, UB + LAG + 2):
                        step(b, more, u)
                    if more:
                        begin(b + 1, True)
                    else:
                        project(b)

                pe.wait_ge(s["xn_ready"], TB)
                for k in range(KD):
                    turn_x(0, k)
                pe.wait_ge(s["w_hi"], 2)
                pe.wait_ge(s["w_lo"], 2)
                for c in range(KD):
                    k_proj(0, c)
                for c in range(KD):
                    q_proj(0, c)
                begin(0, False)
                with pe.Fori(0, B - 1) as b:
                    batch(b, True)
                batch(B - 1, False)

            @block.scalar
            def _(act):
                def ctx_high(b, k):
                    act.wait_ge(s["ctx_in"], b * 16 + 16)
                    nc.scalar.activation(ctx_hi[:, k, :], ctx_t[:, k, :], ACT.Copy).then_inc(s["ctx_hi"], 1)

                def x_high(b, k):
                    act.wait_ge(s["xn_tp"], b * KD + k + 1)
                    nc.scalar.activation(xn_hi[:, k, :], av[k][:], ACT.Copy).then_inc(s["xn_hi"], 1)

                def k_high(b, c):
                    act.wait_ge(s["k_done"], b * KD + c + 1)
                    nc.scalar.activation(k_hi[:, c, :], sc[c][:], ACT.Copy).then_inc(s["k_hi"], 1)

                def q_high(b, c):
                    act.wait_ge(s["q_done"], b * KD + c + 1)
                    nc.scalar.activation(q_hi[:, c, :], av[0][:], ACT.Copy, scale=SCALE).then_inc(s["q_hi"], 1)

                def v_high(b, c):
                    act.wait_ge(s["v_done"], b * 4 + c + 1)
                    nc.scalar.activation(v2[:, 2 * c:2 * c + 2, :, 0:HD],
                                         tp[c % 2][:].rearrange("p (j h d) -> p j h d", h=H, d=HD), ACT.Copy).then_inc(s["v_hi"], 1)

                def exponentials(b, u):
                    w = u % PB
                    act.wait_ge(s["max_done"], b * UB + u + 1)
                    nc.scalar.activation(prob[w][:], prob[w][:], ACT.Exp, scale=-1.0, bias=nmax[:, w:w + 1],
                                         accum_out=rsum[:, w:w + 1]).then_inc(s["exp_done"], 1)

                def high_parts(b, u):
                    t = u % TB
                    for half, done in enumerate(("tp_lo", "tp_hi")):
                        act.wait_ge(s[done], b * UB + u + 1)
                        nc.scalar.activation(pt_hi[:, half * 4:half * 4 + 4, t * P:(t + 1) * P],
                                             tp[half][:].rearrange("p (j i) -> p j i", i=P), ACT.Copy).then_inc(s["pt_hi"], 1)

                def head_low(b, h):
                    act.wait_ge(s["av_done"], b * H + h + 1)
                    act.wait_ge(s["att_ready"], b * H + h + 1)
                    nc.scalar.activation(att_lo[:], av[h % 2][HD:P, :], ACT.Copy).then_inc(s["att_half"], 1)

                def begin(b, before):
                    exponentials(b, 0)
                    if before:
                        head_low(b - 1, H - 1)
                    v_high(b, 0)
                    v_high(b, 1)
                    exponentials(b, 1)
                    exponentials(b, 2)
                    v_high(b, 2)
                    v_high(b, 3)

                def batch(b, more):
                    for u in range(LAG, UB + LAG + 2):
                        if u < UB + LAG:
                            high_parts(b, u - LAG)
                        if u < UB:
                            exponentials(b, u)
                        if more and u in (CTX_STEP - 1, CTX_STEP + 1):
                            ctx_high(b + 1, (u - CTX_STEP + 1) // 2)
                        if more and u - 1 in TURN_X:
                            x_high(b + 1, TURN_X.index(u - 1))
                        if u % TB == 1 and 0 <= u // TB - 2 < H - 1:
                            head_low(b, u // TB - 2)
                        if more and UB <= u < UB + KD:
                            k_high(b + 1, u - UB)
                        if more and UB + LAG - 1 <= u < UB + LAG + 1:
                            q_high(b + 1, u - (UB + LAG - 1))
                    if more:
                        begin(b + 1, True)
                    else:
                        head_low(b, H - 1)

                act.wait_ge(s["w_in"], 48)
                nc.scalar.activation(wkv_hi[:], wkv[:], ACT.Copy).then_inc(s["w_hi"], 1)
                for k in range(KD):
                    ctx_high(0, k)
                nc.scalar.activation(wq_hi[:], wq[:], ACT.Copy).then_inc(s["w_hi"], 1)
                for k in range(KD):
                    x_high(0, k)
                for c in range(KD):
                    k_high(0, c)
                for c in range(KD):
                    q_high(0, c)
                begin(0, False)
                with act.Fori(0, B - 1) as b:
                    batch(b, True)
                batch(B - 1, False)

            @block.vector
            def _(dve):
                dve.sem_inc(s["pt_lo"], 2)
                dve.sem_inc(s["x_ready"], 2)
                dve.sem_inc(s["att_ready"], 1)

                def x_norm(b, t):
                    normalise(nc, m, xn[:, t, :], b * TB + t).then_inc(s["xn_ready"], 1)

                def x_low(b, k):
                    dve.wait_ge(s["xn_hi"], b * KD + k + 1)
                    nc.vector.tensor_tensor(xn_lo[:, k, :], av[k][:], xn_hi[:, k, :], ALU.subtract).then_inc(s["xn_lo"], 1)

                def k_low(b, c):
                    dve.wait_ge(s["k_hi"], b * KD + c + 1)
                    nc.vector.tensor_tensor(k_lo[:, c, :], sc[c][:], k_hi[:, c, :], ALU.subtract).then_inc(s["k_lo"], 1)

                def q_low(b, c):
                    dve.wait_ge(s["q_hi"], b * KD + c + 1)
                    nc.vector.scalar_tensor_tensor(q_lo[:, c, :], av[0][:], SCALE, q_hi[:, c, :],
                                                   ALU.mult, ALU.subtract).then_inc(s["q_lo"], 1)

                def v_low(b, c):
                    dve.wait_ge(s["v_hi"], b * 4 + c + 1)
                    js = slice(2 * c, 2 * c + 2)
                    nc.vector.tensor_tensor(v2[:, js, :, HD:2 * HD], tp[c % 2][:].rearrange("p (j h d) -> p j h d", h=H, d=HD),
                                            v2[:, js, :, 0:HD], ALU.subtract).then_inc(s["v_lo"], 1)

                def maximum(b, u):
                    t, w = u % TB, u % PB
                    dve.wait_ge(s["qk_done"], b * UB + u + 1)
                    dve.wait_ge(s["minf_ready"], b * TB + t + 2)
                    apart(m, dve)
                    nc.vector.tensor_tensor_reduce(out=prob[w][:], in0=sc[u % 2][:], in1=minf[:, t, :], scale=-1.0,
                                                   scalar=BIG, op0=ALU.add, op1=ALU.min,
                                                   accum_out=nmax[:, w:w + 1]).then_inc(s["max_done"], 1)

                def invert(b, u):
                    w = u % PB
                    dve.wait_ge(s["exp_done"], b * UB + u + 1)
                    nc.vector.reciprocal(rinv[:, w:w + 1], rsum[:, w:w + 1]).then_inc(s["inv_done"], 1)

                def low_parts(b, u):
                    t = u % TB
                    for half in range(2):
                        js = slice(half * 4, half * 4 + 4)
                        dve.wait_ge(s["pt_hi"], b * 2 * UB + u * 2 + half + 1)
                        nc.vector.tensor_tensor(pt_lo[:, js, t * P:(t + 1) * P], tp[half][:].rearrange("p (j i) -> p j i", i=P),
                                                pt_hi[:, js, t * P:(t + 1) * P], ALU.subtract).then_inc(s["pt_lo"], 1)

                def head_sum(b, h):
                    dve.wait_ge(s["att_half"], b * H + h + 1)
                    nc.vector.tensor_tensor(att_t[(h % 2) * HD:(h % 2 + 1) * HD, h // 2, :], av[h % 2][0:HD, :], att_lo[:],
                                            ALU.add).then_inc(s["att_ready"], 1)

                def add_projection(b):
                    for half in range(2):
                        dve.wait_ge(s["proj_done"], b * 2 + half + 1)
                        xs = m.x[:, ds(b * TB + 2 * half, 2), :]
                        nc.vector.tensor_tensor(xs, xs, av[half][:].rearrange("p (t d) -> p t d", d=D),
                                                ALU.add).then_inc(s["x_ready"], 1)

                def begin(b, before):
                    maximum(b, 0)
                    if before:
                        head_sum(b - 1, H - 1)
                    v_low(b, 0)
                    maximum(b, 1)
                    invert(b, 0)
                    v_low(b, 1)
                    maximum(b, 2)
                    invert(b, 1)
                    if before:
                        add_projection(b - 1)
                    v_low(b, 2)
                    v_low(b, 3)

                def batch(b, more):
                    for u in range(LAG, UB + LAG + 2):
                        if u < UB:
                            maximum(b, u)
                        if u <= UB:
                            invert(b, u - 1)
                        if u < UB + LAG:
                            low_parts(b, u - LAG)
                        if more and NORM_STEP <= u < NORM_STEP + TB:
                            x_norm(b + 1, u - NORM_STEP)
                        if more and u - 1 in TURN_X:
                            x_low(b + 1, TURN_X.index(u - 1))
                        if u % TB == 2 and 0 <= u // TB - 2 < H - 1:
                            head_sum(b, u // TB - 2)
                        if more and UB <= u < UB + KD:
                            k_low(b + 1, u - UB)
                        if more and UB + LAG - 1 <= u < UB + LAG + 1:
                            q_low(b + 1, u - (UB + LAG - 1))
                    if more:
                        begin(b + 1, True)
                    else:
                        head_sum(b, H - 1)
                        add_projection(b)

                for t in range(TB):
                    x_norm(0, t)
                dve.wait_ge(s["w_hi"], 1)
                nc.vector.tensor_tensor(wkv_lo[:], wkv[:], wkv_hi[:], ALU.subtract).then_inc(s["w_lo"], 1)
                dve.wait_ge(s["w_hi"], 2)
                nc.vector.tensor_tensor(wq_lo[:], wq[:], wq_hi[:], ALU.subtract).then_inc(s["w_lo"], 1)
                for k in range(KD):
                    x_low(0, k)
                for c in range(KD):
                    k_low(0, c)
                for c in range(KD):
                    q_low(0, c)
                begin(0, False)
                with dve.Fori(0, B - 1) as b:
                    batch(b, True)
                batch(B - 1, False)


def experts(nc, m, dram, layer):
    first = layer == 0
    ne = 12 if first else E
    F = 512 if first else 1024
    FC = F // P
    tag = "b_" if first else "d_"
    with ExitStack() as ctx:
        sem = lambda n: nc.alloc_semaphore(name=n)
        sb = lambda n, s, d=F32: ctx.enter_context(nc.sbuf_tensor(tag + n, s, d))
        ps = lambda n, s: ctx.enter_context(nc.psum_tensor(tag + n, s, F32))
        ident = m.const[:, C_IDENT:C_IDENT + P]
        ones = m.const[:, C_ONES:C_ONES + P]
        before = m.const[:, C_BEFORE:C_BEFORE + P]

        w1 = sb("w1", [P, E, KD, F])
        w2 = sb("w2", [P, E, FC, D])
        gate_slot = sb("gate_slot", [P, NBX])
        row_slot = sb("row_slot", [P, NBX], I32)
        expert_of = sb("expert_of", [1, NBX], I32)
        if not first:
            b1 = sb("b1", [P, E, FC])
            b2 = sb("b2", [P, E, D])
            ln_w = sb("ln_w", [P, E, KD])
            ln_b = sb("ln_b", [P, E, KD])
        scratch = ExitStack()
        sr = lambda n, s, d=F32: scratch.enter_context(nc.sbuf_tensor(tag + n, s, d))
        xn_t = [sr(f"xn_t{q}", [P, KD, P]) for q in range(2)]
        gw = sr("gw", [P, KD, ne])
        ebias = sr("ebias", [P, ne])
        logit = sr("logit", [P, ne, T])
        logit2 = sr("logit2", [P, ne, T])
        grid = sr("grid", [P, ne, T])
        pick = [sr(f"pick{k}", [P, ne, T]) for k in range(2)]
        top = [sr(f"top{k}", [P, T]) for k in range(2)]
        idx = [sr(f"idx{k}", [P, T]) for k in range(2)]
        g = [sr(f"g{k}", [P, T]) for k in range(2)]
        zero = [sr(f"zero{k}", [P, T]) for k in range(2)]
        dlog = sr("dlog", [P, T])
        e2 = sr("e2", [P, T])
        den = sr("den", [P, T])
        wz = sr("wz", [P, T])
        load = sr("load", [P, E, T])
        tot = sr("tot", [P, E, T])
        cum = sr("cum", [P, E, T])
        place = sr("place", [P, E, T])
        count = sr("count", [P, E])
        nblk = sr("nblk", [P, E])
        endb = sr("endb", [P, E])
        shift = sr("shift", [P, E])
        pos = [sr(f"pos{k}", [P, T]) for k in range(2)]
        pos_i = [sr(f"pos_i{k}", [P, T], I32) for k in range(2)]
        lane_i = [sr(f"lane_i{k}", [P, T], I32) for k in range(2)]
        lane = [sr(f"lane{k}", [P, T]) for k in range(2)]
        blk_i = [sr(f"blk_i{k}", [P, T], I32) for k in range(2)]
        blk = [sr(f"blk{k}", [P, T]) for k in range(2)]
        in_blk = sr("in_blk", [P, T, NBX])
        val = [sr(f"val{k}", [P, T, 2, NBX]) for k in range(2)]
        in_lane = sr("in_lane", [P, T, P])
        empty = sr("empty", [P, NBX])
        rowf = sr("rowf", [P, NBX])
        bcmp = sr("bcmp", [1, NBX, E])
        bsumf = sr("bsumf", [1, NBX])
        bminf = sr("bminf", [1, NBX])
        alpha = sr("alpha", [P, E])
        xn_all = sr("xn_all", [P, T, D])
        scratch.close()
        xg = [sb(f"xg{q}", [P, D]) for q in range(LANES)]
        rows = [sb(f"rows{q}", [P, 1], I32) for q in range(LANES)]
        add_rows = [sb(f"add_rows{q}", [P, 1], I32) for q in range(LANES)]
        y = [sb(f"y{q}", [P, D]) for q in range(LANES)]
        yb = sb("yb", [P, D])
        xg_t = sb("xg_t", [P, KD, P])
        hid = sb("hid", [P, F])
        hid_t = sb("hid_t", [P, FC, P])

        tpx = [ps(f"tpx{q}", [P, 512]) for q in range(2)]
        hps = ps("hps", [P, 1024])
        hps_t = [ps(f"hps_t{q}", [P, 512]) for q in range(2)]
        yps = ps("yps", [P, 512])
        lps = [yps, ps("mps", [P, 512])]

        acc = dram["acc"] if first else dram["out"]

        names = ("w_in weights_in xn_ready xn_tp xn_t_ready logit_done logit_ready step tot_ready exp_ready "
                 "lane_ready val_ready lane_used xn_out "
                 "bias_in rows_ready add_rows_ready xg_tp xg_t_ready up_done hid_ready hid_tp_lo hid_tp_hi "
                 "hid_t_ready down_done yb_ready y_ready y_free acc_ready added out_done").split()
        s = {n: sem(tag + n) for n in names}
        gathered = [sem(f"{tag}gathered{q}") for q in range(LANES)]

        with nc.Block() as block:
            @block.sync
            def _(sp):
                sp.dma_start(gw[:], dram["gate_0" if first else "gate_1"].rearrange("(k p) e -> p k e", p=P)).then_inc(s["w_in"], 16)
                if first:
                    sp.dma_start(ebias[:], dram["ebias"].partition_broadcast(P)).then_inc(s["w_in"], 16)
                else:
                    sp.dma_start(alpha[:], dram["alpha"].partition_broadcast(P)).then_inc(s["w_in"], 16)
                    sp.dma_start(b1[:], dram["b1"]).then_inc(s["bias_in"], 16)
                    sp.dma_start(b2[:], dram["b2"].partition_broadcast(P)).then_inc(s["bias_in"], 16)
                    sp.dma_start(ln_w[:], dram["ln_w"]).then_inc(s["bias_in"], 16)
                    sp.dma_start(ln_b[:], dram["ln_b"]).then_inc(s["bias_in"], 16)
                for e in range(E):
                    sp.dma_start(w1[:, e, :, :], dram[f"w1_{layer}"][e].rearrange("(k p) f -> p k f", p=P)).then_inc(s["weights_in"], 16)
                    sp.dma_start(w2[:, e, :, :], dram[f"w2_{layer}"][e].rearrange("(c p) d -> p c d", p=P)).then_inc(s["weights_in"], 16)
                sp.wait_ge(s["xn_ready"], T)
                sp.dma_start(dram["rows"][0:T * P, :].rearrange("(t p) d -> p t d", p=P), xn_all[:]).then_inc(s["xn_out"], 16)
                sp.dma_start(dram["rows"][T * P:(T + 1) * P, :], xn_all[:, 0, :]).then_inc(s["xn_out"], 16)
                sp.wait_ge(s["xn_out"], 32)

            @block.tensor
            def _(pe):
                pe.wait_ge(s["w_in"], 32)
                def turn_row(t, q):
                    pe.wait_ge(s["xn_ready"], t + 1)
                    pe.wait_ge(s["xn_t_ready"], t + 1)
                    for k in range(KD):
                        mm = nc.tensor.transpose(tpx[q][:, k * P:(k + 1) * P],
                                                 xn_all[:, t, k * P:(k + 1) * P], ident)
                    mm.then_inc(s["xn_tp"], 1)

                def logits(t, q):
                    pe.wait_ge(s["xn_t_ready"], t + 3)
                    pe.wait_ge(s["logit_ready"], t + 1)
                    for k in range(KD):
                        mm = nc.tensor.matmul(lps[q][:, 0:ne], xn_t[q][:, k, :], gw[:, k, :], start=(k == 0), stop=(k == KD - 1))
                    mm.then_inc(s["logit_done"], 1)

                turn_row(0, 0)
                for t in range(T):
                    if t + 1 < T:
                        turn_row(t + 1, (t + 1) % 2)
                    logits(t, t % 2)
                pe.wait_ge(s["lane_ready"], 1)
                nc.tensor.matmul(yps[:, 0:E * T], before, load[:].rearrange("p e t -> p (e t)"), start=True, stop=True)
                nc.tensor.matmul(yps[:, E * T:2 * E * T], ones, load[:].rearrange("p e t -> p (e t)"),
                                 start=True, stop=True).then_inc(s["tot_ready"], 1)
                for k in range(2):
                    pe.wait_ge(s["val_ready"], k + 1)
                    for half in range(2):
                        pe.wait_ge(s["lane_ready"], 2 * k + half + 2)
                        for t in range(half * T // 2, (half + 1) * T // 2):
                            mm = nc.tensor.matmul(hps[:, 0:2 * NBX], in_lane[:, t, :], val[k][:, t, :, :].rearrange("p a b -> p (a b)"),
                                                  start=(k == 0 and t == 0), stop=(k == 1 and t == T - 1))
                        mm.then_inc(s["lane_used"], 1)

            @block.scalar
            def _(act):
                act.sem_inc(s["xn_t_ready"], 2)
                with act.Fori(0, T // 2) as i:
                    for q in range(2):
                        t = i * 2 + q
                        act.wait_ge(s["xn_tp"], t + 1)
                        nc.scalar.activation(xn_t[q][:], tpx[q][:, 0:D].rearrange("p (k t) -> p k t", k=KD),
                                             ACT.Copy).then_inc(s["xn_t_ready"], 1)
                act.wait_ge(s["exp_ready"], 1)
                nc.scalar.activation(e2[:], dlog[:], ACT.Exp).then_inc(s["exp_ready"], 1)

            @block.vector
            def _(dve):
                dve.sem_inc(s["logit_ready"], 2)
                dve.wait_ge(s["w_in"], 32)
                for t in range(T):
                    normalise(nc, m, xn_all[:, t, :], t).then_inc(s["xn_ready"], 1)
                with dve.Fori(0, T // 2) as i:
                    for q in range(2):
                        t = i * 2 + q
                        dve.wait_ge(s["logit_done"], t + 1)
                        out = logit[:, :, ds(t, 1)].rearrange("p e a -> p (e a)")
                        if first:
                            nc.vector.tensor_tensor(out, lps[q][:, 0:ne], ebias[:], ALU.add).then_inc(s["logit_ready"], 1)
                        else:
                            nc.vector.tensor_copy(out, lps[q][:, 0:ne]).then_inc(s["logit_ready"], 1)

                steps = [0]

                def after(ins):
                    steps[0] += 1
                    ins.then_inc(s["step"], 1)
                    dve.wait_ge(s["step"], steps[0])

                dve.wait_ge(s["logit_ready"], T + 2)
                V = nc.vector
                expert_no = m.const[:, C_EXP:C_EXP + ne * T].rearrange("p (e t) -> p e t", t=T)
                over_e = lambda a: a.rearrange("p e t -> p t e")
                by_e = lambda a, n=ne: a.unsqueeze(1).broadcast_to([P, n, T])
                by_t = lambda a: a.unsqueeze(2).broadcast_to([P, E, T])
                src = logit
                for k in range(2):
                    after(V.tensor_reduce(top[k][:], over_e(src[:]), AX.X, ALU.max))
                    after(V.tensor_tensor(grid[:], src[:], by_e(top[k][:]), ALU.is_equal))
                    after(V.scalar_tensor_tensor(grid[:].rearrange("p e t -> p (e t)"), grid[:].rearrange("p e t -> p (e t)"), -100.0,
                                                 m.const[:, C_EXP:C_EXP + ne * T], ALU.mult, ALU.add))
                    after(V.tensor_reduce(idx[k][:], over_e(grid[:]), AX.X, ALU.min))
                    after(V.tensor_scalar(idx[k][:], idx[k][:], 100.0, None, ALU.add))
                    after(V.tensor_tensor(pick[k][:], expert_no, by_e(idx[k][:]), ALU.is_equal))
                    if k == 0:
                        after(V.scalar_tensor_tensor(logit2[:], pick[0][:], -BIG, logit[:], ALU.mult, ALU.add))
                        src = logit2
                V.tensor_tensor(dlog[:], top[1][:], top[0][:], ALU.subtract).then_inc(s["exp_ready"], 1)
                V.tensor_tensor(load[:], pick[0][:, 0:E, :], pick[1][:, 0:E, :], ALU.add).then_inc(s["lane_ready"], 1)
                dve.wait_ge(s["exp_ready"], 2)
                after(V.tensor_scalar(den[:], e2[:], 1.0, None, ALU.add))
                after(V.reciprocal(g[0][:], den[:]))
                after(V.tensor_tensor(g[1][:], e2[:], g[0][:], ALU.mult))
                if first:
                    for k in range(2):
                        after(V.tensor_scalar(zero[k][:], idx[k][:], E - 0.5, None, ALU.is_gt))
                    after(V.tensor_tensor(wz[:], g[0][:], zero[0][:], ALU.mult))
                    after(V.tensor_tensor(den[:], g[1][:], zero[1][:], ALU.mult))
                    after(V.tensor_tensor(wz[:], wz[:], den[:], ALU.add))
                else:
                    for k in range(2):
                        after(V.tensor_tensor(grid[:], pick[k][:], by_t(alpha[:]), ALU.mult))
                        after(V.tensor_reduce(den[:], over_e(grid[:]), AX.X, ALU.add))
                        after(V.tensor_tensor(g[k][:], g[k][:], den[:], ALU.mult))
                dve.wait_ge(s["tot_ready"], 1)
                flat = lambda a: a.rearrange("p e t -> p (e t)")
                after(V.tensor_copy(flat(tot[:]), yps[:, E * T:2 * E * T]))
                after(V.tensor_tensor_scan(flat(cum[:]), m.const[:, C_ONES:C_ONES + E * T], flat(tot[:]), 0.0, ALU.mult, ALU.add))
                after(V.tensor_reduce(count[:], tot[:], AX.X, ALU.add))
                thr = m.const[:, C_THR:C_THR + T].unsqueeze(1).broadcast_to([P, E, T])
                after(V.tensor_tensor(place[:], by_t(count[:]), thr, ALU.is_gt))
                after(V.tensor_reduce(nblk[:], place[:], AX.X, ALU.add))
                after(V.tensor_tensor_scan(endb[:], m.const[:, C_ONES:C_ONES + E], nblk[:], 0.0, ALU.mult, ALU.add))
                after(V.tensor_tensor(shift[:], endb[:], nblk[:], ALU.subtract))
                after(V.scalar_tensor_tensor(shift[:], shift[:], float(P), count[:], ALU.mult, ALU.add))
                after(V.tensor_tensor(shift[:], shift[:], cum[:, :, T - 1], ALU.subtract))
                after(V.tensor_tensor(place[:], cum[:], tot[:], ALU.subtract))
                after(V.tensor_tensor(flat(place[:]), flat(place[:]), yps[:, 0:E * T], ALU.add))
                after(V.tensor_tensor(place[:], place[:], by_t(shift[:]), ALU.add))
                for k in range(2):
                    after(V.tensor_tensor(cum[:], pick[k][:, 0:E, :], place[:], ALU.mult))
                    after(V.tensor_reduce(pos[k][:], over_e(cum[:]), AX.X, ALU.add))
                    if first:
                        after(V.scalar_tensor_tensor(pos[k][:], zero[k][:], 64.0 * P, pos[k][:], ALU.mult, ALU.add))
                    after(V.tensor_copy(pos_i[k][:], pos[k][:]))
                    after(V.tensor_scalar(lane_i[k][:], pos_i[k][:], P - 1, None, ALU.bitwise_and))
                    after(V.tensor_scalar(blk_i[k][:], pos_i[k][:], 7, None, ALU.arith_shift_right))
                    after(V.tensor_copy(lane[k][:], lane_i[k][:]))
                    after(V.tensor_copy(blk[k][:], blk_i[k][:]))
                block_no = m.const[:, C_BLK:C_BLK + NBX].unsqueeze(1).broadcast_to([P, T, NBX])
                row_no = m.const[:, C_ROW:C_ROW + P].unsqueeze(1).broadcast_to([P, T, P])
                for k in range(2):
                    by_b = lambda a: a.unsqueeze(2).broadcast_to([P, T, NBX])
                    after(V.tensor_tensor(in_blk[:], block_no, by_b(blk[k][:]), ALU.is_equal))
                    after(V.tensor_tensor(val[k][:, :, 0, :], in_blk[:], by_b(m.const[:, C_TOKEN:C_TOKEN + T]), ALU.mult))
                    V.tensor_tensor(val[k][:, :, 1, :], in_blk[:], by_b(g[k][:]), ALU.mult).then_inc(s["val_ready"], 1)
                    dve.wait_ge(s["val_ready"], k + 1)
                    for half in range(2):
                        if k:
                            dve.wait_ge(s["lane_used"], half + 1)
                        h8 = slice(half * T // 2, (half + 1) * T // 2)
                        V.tensor_tensor(in_lane[:, h8, :], row_no[:, h8, :], lane[k][:, h8].unsqueeze(2).broadcast_to([P, T // 2, P]),
                                        ALU.is_equal).then_inc(s["lane_ready"], 1)
                after(V.tensor_tensor(bcmp[:], m.const[0:1, C_BLK:C_BLK + NBX].unsqueeze(2).broadcast_to([1, NBX, E]),
                                      endb[0:1, :].unsqueeze(1).broadcast_to([1, NBX, E]), ALU.is_ge))
                after(V.tensor_reduce(bsumf[:], bcmp[:], AX.X, ALU.add))
                after(V.tensor_scalar(bminf[:], bsumf[:], E - 1.0, None, ALU.min))
                after(V.tensor_copy(expert_of[:], bminf[:]))
                if first:
                    for t in range(T):
                        last = V.scalar_tensor_tensor(m.x[:, t, :], xn_all[:, t, :], wz[:, t:t + 1], m.x[:, t, :], ALU.mult, ALU.add)
                    after(last)
                dve.wait_ge(s["lane_used"], 4)
                after(V.tensor_copy(gate_slot[:], hps[:, NBX:2 * NBX]))
                after(V.tensor_scalar(empty[:], hps[:, 0:NBX], 0.0, None, ALU.is_equal))
                after(V.scalar_tensor_tensor(rowf[:], empty[:], m.const[:, C_PAD:C_PAD + 1], hps[:, 0:NBX], ALU.mult, ALU.add))
                after(V.tensor_scalar(rowf[:], rowf[:], -1.0, None, ALU.add))
                after(V.tensor_copy(row_slot[:], rowf[:]))

        with nc.Block() as block:
            @block.sync
            def _(sp):
                for q in range(LANES):
                    sp.wait_ge(gathered[q], 16)
                sp.dma_start(acc[0:T * P, :].rearrange("(t p) d -> p t d", p=P), m.x[:]).then_inc(s["acc_ready"], 16)
                sp.dma_start(acc[T * P:(T + 1) * P, :], m.x[:, 0, :]).then_inc(s["acc_ready"], 16)
                sp.wait_ge(s["acc_ready"], 32)
                sp.wait_ge(s["added"], 16 * NB)
                if first:
                    sp.dma_start(m.x[:], acc[0:T * P, :].rearrange("(t p) d -> p t d", p=P)).then_inc(s["out_done"], 16)
                    sp.wait_ge(s["out_done"], 16)

            @block.gpsimd
            def _(pool):
                def gather(n, q):
                    nc.gpsimd.tensor_copy(rows[q][:], row_slot[:, ds(n, 1)]).then_inc(s["rows_ready"], 1)
                    pool.wait_ge(s["rows_ready"], n + 1)
                    apart(m, pool)
                    nc.gpsimd.indirect_dma_start(out=xg[q][:], out_offset=None, in_=dram["rows"],
                                                 in_offset=bass.IndirectOffsetOnAxis(ap=rows[q][:], axis=0)).then_inc(gathered[q], 16)

                def add(n, q):
                    nc.gpsimd.tensor_copy(add_rows[q][:], row_slot[:, ds(n, 1)]).then_inc(s["add_rows_ready"], 1)
                    pool.wait_ge(s["add_rows_ready"], n + 1)
                    pool.wait_ge(s["y_ready"], n + 2)
                    if isinstance(n, int) and n == 0:
                        pool.wait_ge(s["acc_ready"], 32)
                    else:
                        pool.wait_ge(s["added"], n * 16)
                        pool.sem_inc(s["y_free"], 1)
                    nc.gpsimd.indirect_dma_start(out=acc, out_offset=bass.IndirectOffsetOnAxis(ap=add_rows[q][:], axis=0),
                                                 in_=y[q][:], in_offset=None, compute_op=ALU.add).then_inc(s["added"], 16)

                def next_block(i, q):
                    n = i * LANES + q
                    pool.wait_ge(s["xg_tp"], n + 1)
                    pool.wait_ge(gathered[q], i * 16 + 16)
                    gather(n + LANES, q)
                    add(n, q)

                for q in range(LANES):
                    gather(q, q)
                for q in range(LANES):
                    next_block(0, q)
                with pool.Fori(1, NB // LANES - 1) as i:
                    for q in range(LANES):
                        next_block(i, q)
                for q in range(LANES):
                    add(NB - LANES + q, q)

            @block.tensor
            def _(pe):
                pe.wait_ge(s["weights_in"], 16 * 2 * E)

                def expert(n):
                    return pe.value_load(expert_of[0:1, ds(n, 1)], min_val=0, max_val=E - 1)

                def turn_in(n, q, turn):
                    pe.wait_ge(gathered[q], turn * 16 + 16)
                    pe.wait_ge(s["xg_t_ready"], n + 1)
                    for k in range(KD):
                        mm = nc.tensor.transpose(tpx[0][:, k * P:(k + 1) * P], xg[q][:, k * P:(k + 1) * P], ident)
                    mm.then_inc(s["xg_tp"], 1)

                def up(n):
                    e = expert(n)
                    pe.wait_ge(s["xg_t_ready"], n + 2)
                    pe.wait_ge(s["hid_ready"], n + 1)
                    for c in range(F // 512):
                        for k in range(KD):
                            mm = nc.tensor.matmul(hps[:, c * 512:(c + 1) * 512], xg_t[:, k, :],
                                                  w1[:, ds(e, 1), k, c * 512:(c + 1) * 512].rearrange("p a f -> p (a f)"),
                                                  start=(k == 0), stop=(k == KD - 1))
                    mm.then_inc(s["up_done"], 1)

                def turn_hidden(n):
                    pe.wait_ge(s["hid_ready"], n + 2)
                    for half, done in enumerate(("hid_tp_lo", "hid_tp_hi")):
                        pe.wait_ge(s["hid_t_ready"], n * 2 + half + 1)
                        for c in range(FC // 2):
                            at = half * (FC // 2) + c
                            mm = nc.tensor.transpose(hps_t[half][:, c * P:(c + 1) * P], hid[:, at * P:(at + 1) * P], ident)
                        mm.then_inc(s[done], 1)

                def down(n):
                    e = expert(n)
                    pe.wait_ge(s["yb_ready" if not first else "y_ready"], n + 1)
                    for c in range(FC):
                        if c % (FC // 2) == 0:
                            pe.wait_ge(s["hid_t_ready"], n * 2 + c // (FC // 2) + 3)
                        mm = nc.tensor.matmul(yps[:, 0:D], hid_t[:, c, :], w2[:, ds(e, 1), c, :].rearrange("p a d -> p (a d)"),
                                              start=(c == 0), stop=(c == FC - 1))
                    mm.then_inc(s["down_done"], 1)

                turn_in(0, 0, 0)
                up(0)
                turn_in(1, 1, 0)
                with pe.Fori(0, NB // LANES - 1) as i:
                    for q in range(LANES):
                        n = i * LANES + q
                        turn_hidden(n)
                        up(n + 1)
                        turn_in(n + 2, (q + 2) % LANES, i + (q + 2) // LANES)
                        down(n)
                for q in range(LANES):
                    n = NB - LANES + q
                    turn_hidden(n)
                    if q + 1 < LANES:
                        up(n + 1)
                    if q + 2 < LANES:
                        turn_in(n + 2, q + 2, NB // LANES - 1)
                    down(n)

            @block.scalar
            def _(act):
                act.sem_inc(s["hid_t_ready"], 2)
                if not first:
                    act.wait_ge(s["bias_in"], 64)
                with act.Fori(0, LANES) as i:
                    for q in range(NB // LANES):
                        n = i * (NB // LANES) + q
                        if not first:
                            e = act.value_load(expert_of[0:1, ds(n, 1)], min_val=0, max_val=E - 1)
                        for half in range(2):
                            src = hps_t[half][:, 0:F // 2].rearrange("p (c t) -> p c t", t=P)
                            c0 = half * (FC // 2)
                            if half == 0:
                                act.wait_ge(s["hid_tp_lo"], n + 1)
                            else:
                                act.wait_ge(s["hid_tp_hi"], n + 2)
                            if first:
                                op = nc.scalar.activation(hid_t[:, c0:c0 + FC // 2, :], src, ACT.Silu)
                            else:
                                for c in range(FC // 2):
                                    op = nc.scalar.activation(hid_t[:, c0 + c, :], src[:, c, :], ACT.Gelu_apprx_tanh,
                                                              bias=b1[:, ds(e, 1), c0 + c])
                            op.then_inc(s["hid_t_ready"], 1)

            @block.vector
            def _(dve):
                for credit in ("xg_t_ready", "hid_ready", "hid_tp_hi", "yb_ready", "y_ready"):
                    dve.sem_inc(s[credit], 1)
                dve.sem_inc(s["y_free"], LANES)
                if not first:
                    dve.wait_ge(s["bias_in"], 64)

                def expert(n):
                    return None if first else dve.value_load(expert_of[0:1, ds(n, 1)], min_val=0, max_val=E - 1)

                def take_in(n):
                    e = expert(n)
                    dve.wait_ge(s["xg_tp"], n + 1)
                    if first:
                        nc.vector.tensor_copy(xg_t[:], tpx[0][:, 0:D].rearrange("p (k t) -> p k t", k=KD)).then_inc(s["xg_t_ready"], 1)
                    else:
                        for k in range(KD):
                            op = nc.vector.tensor_scalar(xg_t[:, k, :], tpx[0][:, k * P:(k + 1) * P],
                                                         ln_w[:, ds(e, 1), k], ln_b[:, ds(e, 1), k], ALU.mult, ALU.add)
                        op.then_inc(s["xg_t_ready"], 1)

                def take_hidden(n):
                    dve.wait_ge(s["up_done"], n + 1)
                    dve.wait_ge(s["hid_tp_hi"], n + 1)
                    nc.vector.tensor_copy(hid[:], hps[:, 0:F]).then_inc(s["hid_ready"], 1)

                def result(n, q):
                    e = expert(n)
                    dve.wait_ge(s["down_done"], n + 1)
                    dve.wait_ge(s["y_free"], n + 1)
                    gate = gate_slot[:, ds(n, 1)]
                    if first:
                        nc.vector.tensor_scalar(y[q][:], yps[:, 0:D], gate, None, ALU.mult).then_inc(s["y_ready"], 1)
                    else:
                        dve.wait_ge(s["y_ready"], n + 1)
                        nc.vector.tensor_tensor(yb[:], yps[:, 0:D], b2[:, ds(e, 1), :].rearrange("p a d -> p (a d)"),
                                                ALU.add).then_inc(s["yb_ready"], 1)
                        dve.wait_ge(s["yb_ready"], n + 2)
                        nc.vector.tensor_scalar(y[q][:], yb[:], gate, None, ALU.mult).then_inc(s["y_ready"], 1)

                take_in(0)
                take_hidden(0)
                take_in(1)
                with dve.Fori(0, NB // LANES - 1) as i:
                    for q in range(LANES):
                        n = i * LANES + q
                        take_hidden(n + 1)
                        take_in(n + 2)
                        result(n, q)
                for q in range(LANES):
                    n = NB - LANES + q
                    if q + 1 < LANES:
                        take_hidden(n + 1)
                    if q + 2 < LANES:
                        take_in(n + 2)
                    result(n, q)


def build(nc, dram):
    m = Mem()
    with ExitStack() as top:
        m.sem = lambda name: top.enter_context(nc.semaphore(name))
        sb = lambda n, s, d=F32: top.enter_context(nc.sbuf_tensor(n, s, d))
        m.x = sb("x", [P, T, D])
        m.const = sb("const", [P, C_END])
        m.bn = sb("bn", [P, T, 6])
        m.mean2, m.diff, m.m2, m.mean, m.dd, m.var, m.std, m.rstd = (
            sb(n, [P, T]) for n in "mean2 diff m2 mean dd var std rstd".split())
        m.nc = nc
        m.s_apart = [m.sem("apart_pool"), m.sem("apart_dve")]
        m.s_const = m.sem("const_in")
        load_phase(nc, m, dram)
        for tag, phase in (("n0", lambda: attention0(nc, m, dram)), ("n1", lambda: experts(nc, m, dram, 0)),
                           ("n2", lambda: attention1(nc, m, dram)), ("n3", lambda: experts(nc, m, dram, 1))):
            layer_norm_stats(nc, m, tag)
            with nc.cleanup_on_exit():
                phase()


def kernel(x, ctx_1024, mask_BxSxS2_bf1, L0_xattn_w_sim, L0_xattn_b_sim, L0_xattn_W_qv, L0_xattn_b_qv,
           L0_ffn_gate_w, L0_ffn_expert_bias, L0_ffn_w1, L0_ffn_w2, L1_xattn_Wq, L1_xattn_Wkv, L1_xattn_Wo,
           L1_ffn_Wg, L1_ffn_alpha, L1_ffn_ln_w, L1_ffn_ln_b, L1_ffn_fc1_w, L1_ffn_fc1_b, L1_ffn_fc2_w, L1_ffn_fc2_b):
    import concourse.bacc as bacc
    from concourse.bass_utils import run_bass_kernel_spmd

    arr = lambda a: np.ascontiguousarray(np.asarray(a))
    ctx = arr(ctx_1024).reshape(B * M, D)
    host = {
        "x": arr(x).reshape(B * S, D),
        "const": shape_constants(),
        "ctx": ctx,
        "ctx_t": arr(ctx.T),
        "mask": arr(mask_BxSxS2_bf1).reshape(B * S, M).view(np.uint8),
        "w_sim": arr(arr(L0_xattn_w_sim).reshape(3 * KD, P).T),
        "b_sim": arr(L0_xattn_b_sim),
        "W_qv": arr(L0_xattn_W_qv),
        "b_qv": arr(L0_xattn_b_qv),
        "gate_0": arr(arr(L0_ffn_gate_w).T),
        "ebias": arr(L0_ffn_expert_bias),
        "w1_0": arr(arr(L0_ffn_w1).transpose(0, 2, 1)),
        "w2_0": arr(arr(L0_ffn_w2).transpose(0, 2, 1)),
        "Wq": arr(L1_xattn_Wq),
        "Wkv": arr(L1_xattn_Wkv),
        "Wo": arr(L1_xattn_Wo),
        "gate_1": arr(L1_ffn_Wg),
        "alpha": arr(L1_ffn_alpha),
        "ln_w": arr(arr(L1_ffn_ln_w).reshape(E, KD, P).transpose(2, 0, 1)),
        "ln_b": arr(arr(L1_ffn_ln_b).reshape(E, KD, P).transpose(2, 0, 1)),
        "w1_1": arr(L1_ffn_fc1_w),
        "b1": arr(arr(L1_ffn_fc1_b).reshape(E, -1, P).transpose(2, 0, 1)),
        "w2_1": arr(L1_ffn_fc2_w),
        "b2": arr(L1_ffn_fc2_b),
    }
    nc = bacc.Bacc("TRN2", target_bir_lowering=False, num_devices=1)
    dram = {n: nc.dram_tensor(f"in_{n}", a.shape, mybir.dt.from_np(a.dtype), kind="ExternalInput").ap()
            for n, a in host.items()}
    dram["rows"] = nc.dram_tensor("rows", [(T + 1) * P, D], F32, kind="Internal").ap()
    dram["acc"] = nc.dram_tensor("acc", [(T + 1) * P, D], F32, kind="Internal").ap()
    dram["out"] = nc.dram_tensor("out_x", [(T + 1) * P, D], F32, kind="ExternalOutput").ap()
    build(nc, dram)
    r = run_bass_kernel_spmd(nc, [{f"in_{n}": a for n, a in host.items()}], core_ids=[0])
    return r.results[0]["out_x"][0:B * S].reshape(B, S, D)
```
